# Optimizing a Trainium2 kernel written in Bass

```python
import numpy as np
import jax
import jax.numpy as jnp

def _softmax(x, axis=-1):
    return jax.nn.softmax(x, axis=axis)

def _gelu(x):
    return jax.nn.gelu(x, approximate=True)

def _silu(x):
    return jax.nn.silu(x)

def _sigmoid(x):
    return jax.nn.sigmoid(x)

def _layernorm(x, axis=-1, eps=1e-05):
    m = jnp.mean(x, axis=axis, keepdims=True)
    v = jnp.var(x, axis=axis, keepdims=True)
    return (x - m) / jnp.sqrt(v + eps)

def _scatter_add(tgt, idx, src, axis=0):
    return tgt.at[idx].add(src)

def _segment_sum(src, seg, n):
    return jax.ops.segment_sum(src, seg, n)
kernel_name = 'mk_prb_d1_jaxref_r8_732617'

def setup_inputs(seed: int=0):
    np.random.seed(seed)
    _w = jnp.asarray

    def _L0_attn_setup():
        import math
        import jax, jax.numpy as jnp
        import numpy as np
        HEAD_DIM = 128
        NUM_HEADS = 16
        ROPE_BASE = 10000.0

        def _rope_tables(seq_len, dim, dtype):
            inv_freq = 1.0 / ROPE_BASE ** (jnp.arange(0, dim, 2, dtype=jnp.float32) / dim)
            t = jnp.arange(seq_len, dtype=jnp.float32)
            freqs = jnp.einsum('i,j->ij', t, inv_freq)
            emb = jnp.concatenate([freqs, freqs], axis=-1)
            return (jnp.cos(emb).astype(dtype), jnp.sin(emb).astype(dtype))

        def _rotate_half(x):
            x1, x2 = jnp.split(x, 2, axis=-1)
            return jnp.concatenate([-x2, x1], axis=-1)

        def _apply_rope(x, cos, sin):
            return x * cos[None, :, None, :] + _rotate_half(x) * sin[None, :, None, :]
        key = jax.random.key(seed)
        k1, k2, k3 = jax.random.split(key, 3)
        B, S, dim = (2, 256, 256)
        out_dim = (NUM_HEADS + 2 * NUM_HEADS) * HEAD_DIM
        x = jax.random.normal(k1, (B, S, dim), dtype=jnp.float32)
        w_qkv = jax.random.normal(k2, (out_dim, dim), dtype=jnp.float32) * 0.02
        w_out = jax.random.normal(k3, (dim, NUM_HEADS * HEAD_DIM), dtype=jnp.float32) * 0.02
        return {'x': x, 'w_qkv': w_qkv, 'w_out': w_out}
    _L0_attn_in = _L0_attn_setup()

    def _L0_ffn_setup():
        import jax, jax.numpy as jnp
        import numpy as np
        BLOCK_SIZE = 32
        FP4_GRID = jnp.array([0.0, 0.5, 1.0, 1.5, 2.0, 3.0, 4.0, 6.0], dtype=jnp.float32)
        FP4_MIDS = jnp.array([0.25, 0.75, 1.25, 1.75, 2.5, 3.5, 5.0], dtype=jnp.float32)

        def quantize_to_mxfp4(w, block_size=BLOCK_SIZE):
            K, N = w.shape
            wb = w.reshape(K // block_size, block_size, N)
            amax = jnp.max(jnp.abs(wb), axis=1, keepdims=True)
            exp = jnp.floor(jnp.log2(jnp.maximum(amax, 1e-30))) - 2.0
            scales = jnp.exp2(exp)
            x = wb / scales
            idx = jnp.digitize(jnp.abs(x), FP4_MIDS)
            q = jnp.sign(x) * FP4_GRID[idx]
            return (q, scales)

        def mxfp4_matmul(inputs, q, scales, block_size=BLOCK_SIZE):
            K = inputs.shape[-1]
            N = q.shape[-1]
            w = (q * scales).reshape(K, N)
            return inputs @ w
        key = jax.random.key(seed)
        ks = jax.random.split(key, 3)
        B, S, D, F = (4, 256, 256, 1024)
        inputs = jax.random.normal(ks[0], (B, S, D), dtype=jnp.float32)
        up_kernel = jax.random.normal(ks[1], (D, F), dtype=jnp.float32) * (1.0 / np.sqrt(D))
        down_kernel = jax.random.normal(ks[2], (F, D), dtype=jnp.float32) * (1.0 / np.sqrt(F))
        up_bias = jnp.zeros((F,), dtype=jnp.float32)
        down_bias = jnp.zeros((D,), dtype=jnp.float32)
        return {'inputs': inputs, 'up_kernel': up_kernel, 'up_bias': up_bias, 'down_kernel': down_kernel, 'down_bias': down_bias}
    _L0_ffn_in = _L0_ffn_setup()
    _d = {'L0_attn_x': _L0_attn_in['x'], 'L0_attn_w_qkv': _L0_attn_in['w_qkv'], 'L0_attn_w_out': _L0_attn_in['w_out'], 'L0_ffn_up_kernel': _L0_ffn_in['up_kernel'], 'L0_ffn_up_bias': _L0_ffn_in['up_bias'], 'L0_ffn_down_kernel': _L0_ffn_in['down_kernel'], 'L0_ffn_down_bias': _L0_ffn_in['down_bias']}
    _x0 = _d['L0_attn_x']
    _d['L0_attn_x'] = jax.random.normal(jax.random.fold_in(jax.random.key(seed), 1), (4, 1024, 256), dtype=_x0.dtype)
    del _x0
    return _d

def reference(L0_attn_x, L0_attn_w_qkv, L0_attn_w_out, L0_ffn_up_kernel, L0_ffn_up_bias, L0_ffn_down_kernel, L0_ffn_down_bias):

    def _L0_attn_ref(x, w_qkv, w_out):
        import math
        import jax, jax.numpy as jnp
        import numpy as np
        HEAD_DIM = 128
        NUM_HEADS = 16
        ROPE_BASE = 10000.0

        def _rope_tables(seq_len, dim, dtype):
            inv_freq = 1.0 / ROPE_BASE ** (jnp.arange(0, dim, 2, dtype=jnp.float32) / dim)
            t = jnp.arange(seq_len, dtype=jnp.float32)
            freqs = jnp.einsum('i,j->ij', t, inv_freq)
            emb = jnp.concatenate([freqs, freqs], axis=-1)
            return (jnp.cos(emb).astype(dtype), jnp.sin(emb).astype(dtype))

        def _rotate_half(x):
            x1, x2 = jnp.split(x, 2, axis=-1)
            return jnp.concatenate([-x2, x1], axis=-1)

        def _apply_rope(x, cos, sin):
            return x * cos[None, :, None, :] + _rotate_half(x) * sin[None, :, None, :]
        B, S, _ = x.shape
        H, D = (NUM_HEADS, HEAD_DIM)
        qkv = jnp.einsum('bsd,od->bso', x, w_qkv)
        qkv = qkv.reshape(B, S, 3 * H, D)
        q = qkv[:, :, :H, :]
        k = qkv[:, :, H:2 * H, :]
        v = qkv[:, :, 2 * H:, :]
        cos, sin = _rope_tables(S, D, x.dtype)
        q = _apply_rope(q, cos, sin)
        k = _apply_rope(k, cos, sin)
        scale = 1.0 / math.sqrt(D)
        logits = jnp.einsum('bqhd,bkhd->bhqk', q, k) * scale
        attn = jax.nn.softmax(logits.astype(jnp.float32), axis=-1).astype(logits.dtype)
        out = jnp.einsum('bhqk,bkhd->bqhd', attn, v)
        out = out.reshape(B, S, H * D)
        return jnp.einsum('bso,do->bsd', out, w_out)

    def _L0_ffn_ref(inputs, up_kernel, up_bias, down_kernel, down_bias):
        import jax, jax.numpy as jnp
        import numpy as np
        BLOCK_SIZE = 32
        FP4_GRID = jnp.array([0.0, 0.5, 1.0, 1.5, 2.0, 3.0, 4.0, 6.0], dtype=jnp.float32)
        FP4_MIDS = jnp.array([0.25, 0.75, 1.25, 1.75, 2.5, 3.5, 5.0], dtype=jnp.float32)

        def quantize_to_mxfp4(w, block_size=BLOCK_SIZE):
            K, N = w.shape
            wb = w.reshape(K // block_size, block_size, N)
            amax = jnp.max(jnp.abs(wb), axis=1, keepdims=True)
            exp = jnp.floor(jnp.log2(jnp.maximum(amax, 1e-30))) - 2.0
            scales = jnp.exp2(exp)
            x = wb / scales
            idx = jnp.digitize(jnp.abs(x), FP4_MIDS)
            q = jnp.sign(x) * FP4_GRID[idx]
            return (q, scales)

        def mxfp4_matmul(inputs, q, scales, block_size=BLOCK_SIZE):
            K = inputs.shape[-1]
            N = q.shape[-1]
            w = (q * scales).reshape(K, N)
            return inputs @ w
        q_up, s_up = quantize_to_mxfp4(up_kernel, BLOCK_SIZE)
        x = mxfp4_matmul(inputs, q_up, s_up, BLOCK_SIZE) + up_bias
        x = jax.nn.gelu(x)
        q_dn, s_dn = quantize_to_mxfp4(down_kernel, BLOCK_SIZE)
        x = mxfp4_matmul(x, q_dn, s_dn, BLOCK_SIZE) + down_bias
        return x
    x = L0_attn_x
    xn = _layernorm(x, axis=-1)
    x = x + _L0_attn_ref(xn, L0_attn_w_qkv, L0_attn_w_out) + _L0_ffn_ref(xn, L0_ffn_up_kernel, L0_ffn_up_bias, L0_ffn_down_kernel, L0_ffn_down_bias)
    return x

_drawn_inputs = setup_inputs


def setup_inputs(seed=0):
    import zlib

    import numpy as np

    out = dict(_drawn_inputs(seed))
    spreads = {'L0_ffn_up_bias': (0.0, 0.8), 'L0_ffn_down_bias': (0.0, 0.8)}
    factors = {'L0_attn_w_qkv': 7.659, 'L0_attn_w_out': 7.894}
    for name, (base, spread) in spreads.items():
        noise = np.random.default_rng([zlib.crc32(name.encode()), seed]).standard_normal(out[name].shape)
        drawn = base * np.exp(spread * noise) if base else spread * noise
        out[name] = jnp.asarray(drawn.astype(out[name].dtype))
    for name, factor in factors.items():
        out[name] = (out[name] * factor).astype(out[name].dtype)
    return out
```

```python
import math
from contextlib import ExitStack

import numpy as np

import concourse.bass as bass
from concourse import mybir

F32 = mybir.dt.float32
F32R = mybir.dt.float32r
U32 = mybir.dt.uint32
ACT = mybir.ActivationFunctionType
ALU = mybir.AluOpType
AXX = mybir.AxisListType.X

BATCH, SEQ, DIM = 4, 1024, 256
HEADS, HEAD = 16, 128
FF = 1024
P = 128
TOK = BATCH * SEQ
TILES = TOK // P
BT = SEQ // P
CT = DIM // P
FT = FF // P
BLOCK = 32
SCALE = 1.0 / math.sqrt(HEAD)
EPS = 1e-5
HALF = SEQ // 2
PAIRS = BATCH * HEADS // 2
PAIRS_PER_SEQ = HEADS // 2
CHUNK = 2 * P
WCOLS = 6 * HEAD


def stage_one(nc, d):
    with ExitStack() as ctx:
        def sb(name, shape, dt=F32):
            return ctx.enter_context(nc.sbuf_tensor(name, shape, dt))

        def sem(name):
            return ctx.enter_context(nc.semaphore(name))

        ident = sb("ident1", [P, P])
        x_all = sb("x_all", [P, TILES, DIM])
        xn = sb("xn", [P, BT, DIM])
        square = sb("square", [P, DIM])
        neg_mean = sb("neg_mean", [P, TILES])
        sum_sq = sb("sum_sq", [P, TILES])
        var = sb("var", [P, TILES])
        rstd0 = sb("rstd0", [P, TILES])
        rstd = sb("rstd", [P, TILES])
        newton = sb("newton", [P, TILES])
        minus_half = sb("minus_half", [P, TILES])
        xnt_hi = sb("xnt_hi", [P, CT, TOK], F32R)
        xnt_lo = sb("xnt_lo", [P, CT, TOK], F32R)
        w_rows = [sb("up_rows", [P, FT * DIM]), sb("down_rows", [P, CT * FF])]
        w_abs = sb("w_abs", [P, 2048])
        w_acc = sb("w_acc", [P, 2048])
        amax = sb("amax", [P, 2048 // BLOCK])
        scale_half = sb("scale_half", [P, 2048 // BLOCK])
        inv_scale = sb("inv_scale", [P, 2048 // BLOCK])
        up_w = sb("up_w", [P, CT, FF], F32R)
        down_w = sb("down_w", [P, FT, DIM], F32R)
        up_bias = sb("up_bias", [P, FT])
        down_bias = sb("down_bias", [P, DIM])
        g_full = sb("g_full", [P, 2, HALF])
        g_hi = sb("g_hi", [P, 4, HALF], F32R)
        g_lo = sb("g_lo", [P, 4, HALF], F32R)
        y_out = sb("y_out", [P, 2, 4, DIM])
        bank = [ctx.enter_context(nc.psum_tensor(f"bankA{i}", [P, 512], F32)) for i in range(2)]
        y_ps = ctx.enter_context(nc.psum_tensor("y_ps", [P, 4, 512], F32))

        x_loaded = [sem(f"x_loaded{b}") for b in range(BATCH)]
        small_loaded = sem("small_loaded")
        rows_loaded = [sem("up_rows_loaded"), sem("down_rows_loaded")]
        mean_ready = sem("mean_ready")
        squares_ready = sem("squares_ready")
        var_ready = sem("var_ready")
        guess_ready = sem("guess_ready")
        half_ready = sem("half_ready")
        xn_ready = sem("xn_ready")
        xt_ready = sem("xt_ready")
        xt_hi_ready = sem("xt_hi_ready")
        xt_lo_ready = sem("xt_lo_ready")
        xb_ready = sem("xb_ready")
        vchain = sem("vchain")
        quant_ready = sem("quant_ready")
        wt_ready = sem("wt_ready")
        wt_copied = sem("wt_copied")
        up_ready = sem("up_ready")
        gelu_ready = sem("gelu_ready")
        g_hi_ready = sem("g_hi_ready")
        g_lo_ready = sem("g_lo_ready")
        down_ready = sem("down_ready")
        y_ready = sem("y_ready")
        y_stored = [sem(f"y_stored{s}") for s in range(2)]
        xt_stored = sem("xt_stored")

        block = ctx.enter_context(nc.Block())
        GROUPS = TOK // HALF

        @block.sync
        def _(sp):
            for b in range(BATCH):
                sp.dma_start(x_all[:, b * BT:(b + 1) * BT, :], d["x"][b]).then_inc(x_loaded[b], 16)
                if b == 0:
                    sp.dma_start(ident[:, :], d["ident"]).then_inc(small_loaded, 16)
                    sp.dma_start(up_bias[:, :], d["up_bias"]).then_inc(small_loaded, 16)
                    sp.dma_start(down_bias[:, :], d["down_bias"].to_broadcast([P, DIM])).then_inc(small_loaded, 16)
            for n, name in enumerate(("up_rows", "down_rows")):
                sp.dma_start(w_rows[n][:, :], d[name]).then_inc(rows_loaded[n], 16)
            for b in range(BATCH):
                sp.wait_ge(xt_lo_ready, 4 * (b + 1))
                cols = slice(b * SEQ, (b + 1) * SEQ)
                sp.dma_start(d["xnt"][0, :, :, cols], xnt_hi[:, :, cols].bitcast(F32)).then_inc(xt_stored, 16)
                sp.dma_start(d["xnt"][1, :, :, cols], xnt_lo[:, :, cols].bitcast(F32)).then_inc(xt_stored, 16)
            with sp.Fori(0, GROUPS // 2) as g2:
                for s in range(2):
                    sp.wait_ge(y_ready, g2 * 2 + s + 1)
                    sp.dma_start(d["y"][:, bass.ds(g2 * 8 + 4 * s, 4), :], y_out[:, s, :, :]).then_inc(y_stored[s], 16)
            for s in range(2):
                sp.wait_ge(y_stored[s], 16 * (GROUPS // 2))
            sp.wait_ge(xt_stored, 32 * BATCH)

        @block.gpsimd
        def _(pool):
            nc.gpsimd.memset(minus_half[:, :], -0.5).then_inc(half_ready, 1)
            pool.wait_ge(half_ready, 1)
            for b in range(BATCH):
                t = slice(b * BT, (b + 1) * BT)
                pool.wait_ge(var_ready, b + 1)
                nc.gpsimd.tensor_tensor(rstd0[:, t], var[:, t], minus_half[:, t], ALU.pow).then_inc(guess_ready, 1)
            pool.wait_ge(small_loaded, 48)
            for b in range(BATCH):
                pool.wait_ge(xn_ready, b + 1)
                for t in range(b * BT, (b + 1) * BT):
                    nc.gpsimd.tensor_tensor(x_all[:, t, :], x_all[:, t, :], down_bias[:, :], ALU.add).then_inc(xb_ready, 1)

        @block.scalar
        def _(act):
            for b in range(BATCH):
                act.wait_ge(mean_ready, b + 1)
                for t in range(b * BT, (b + 1) * BT):
                    nc.scalar.activation(square[:, :], x_all[:, t, :], ACT.Square, bias=neg_mean[:, t:t + 1],
                                         accum_out=sum_sq[:, t:t + 1]).then_inc(squares_ready, 1)
                    act.wait_ge(squares_ready, t + 1)
                for n in range(4):
                    act.wait_ge(xt_ready, 4 * b + n + 1)
                    c, h = n // 2, n % 2
                    cols = slice(b * SEQ + h * HALF, b * SEQ + (h + 1) * HALF)
                    nc.scalar.activation(xnt_hi[:, c, cols], bank[n % 2][:, :], ACT.Copy).then_inc(xt_hi_ready, 1)
            for n in range(8):
                act.wait_ge(wt_ready, n + 1)
                if n < 4:
                    dst = up_w[:, n // 2, (n % 2) * 512:(n % 2 + 1) * 512]
                else:
                    dst = down_w[:, 2 * (n - 4):2 * (n - 4) + 2, :].rearrange("p a b -> p (a b)")
                nc.scalar.activation(dst, bank[n % 2][:, :], ACT.Copy).then_inc(wt_copied, 1)

            def gelu(g, f):
                act.wait_ge(up_ready, g * FT + f + 1)
                if f >= 2:
                    act.wait_ge(g_lo_ready, g * FT + (f - 1))
                else:
                    act.wait_ge(g_lo_ready, g * FT + (f - 1) + 0) if not isinstance(g, int) else None
                nc.scalar.activation(g_full[:, f % 2, :], bank[f % 2][:, :], ACT.Gelu_apprx_tanh,
                                     bias=up_bias[:, f:f + 1]).then_inc(gelu_ready, 1)

            for f in range(FT):
                gelu(0, f)
            with act.Fori(1, GROUPS) as g:
                for f in range(FT):
                    gelu(g, f)

        @block.vector
        def _(dve):
            chain = [0]

            def link(ins):
                chain[0] += 1
                ins.then_inc(vchain, 1)
                dve.wait_ge(vchain, chain[0])

            def statistics(b):
                t = slice(b * BT, (b + 1) * BT)
                dve.wait_ge(x_loaded[b], 16)
                link(nc.vector.tensor_reduce(neg_mean[:, t], x_all[:, t, :], AXX, ALU.add))
                nc.vector.tensor_scalar(neg_mean[:, t], neg_mean[:, t], -1.0 / DIM, None,
                                        ALU.mult).then_inc(mean_ready, 1)

            def normalise(b):
                t = slice(b * BT, (b + 1) * BT)
                dve.wait_ge(squares_ready, (b + 1) * BT)
                nc.vector.tensor_scalar(var[:, t], sum_sq[:, t], 1.0 / DIM, EPS, ALU.mult, ALU.add).then_inc(var_ready, 1)
                dve.wait_ge(guess_ready, b + 1)
                link(nc.vector.tensor_tensor(newton[:, t], rstd0[:, t], rstd0[:, t], ALU.mult))
                link(nc.vector.tensor_tensor(newton[:, t], newton[:, t], var[:, t], ALU.mult))
                link(nc.vector.tensor_scalar(newton[:, t], newton[:, t], -0.5, 1.5, ALU.mult, ALU.add))
                link(nc.vector.tensor_tensor(rstd[:, t], rstd0[:, t], newton[:, t], ALU.mult))
                if b >= 1:
                    dve.wait_ge(xt_ready, 4 * b)
                for i in range(BT):
                    n = b * BT + i
                    last = nc.vector.tensor_scalar(xn[:, i, :], x_all[:, n, :], neg_mean[:, n:n + 1],
                                                   rstd[:, n:n + 1], ALU.add, ALU.mult)
                last.then_inc(xn_ready, 1)

            def low_parts(b):
                for n in range(4):
                    dve.wait_ge(xt_hi_ready, 4 * b + n + 1)
                    c, h = n // 2, n % 2
                    cols = slice(b * SEQ + h * HALF, b * SEQ + (h + 1) * HALF)
                    nc.vector.tensor_tensor(xnt_lo[:, c, cols], bank[n % 2][:, :], xnt_hi[:, c, cols].bitcast(F32),
                                            ALU.subtract).then_inc(xt_lo_ready, 1)

            def quantise(n):
                rows = w_rows[n]
                blocks = lambda a: a[:, :].rearrange("p (a b) -> p a b", b=BLOCK)
                wide = lambda a: a[:, :].rearrange("p (a o) -> p a o", o=1).to_broadcast([P, 2048 // BLOCK, BLOCK])
                dve.wait_ge(rows_loaded[n], 16)
                nc.vector.tensor_scalar(w_abs[:, :].bitcast(U32), rows[:, :].bitcast(U32), 0x7FFFFFFF, None,
                                        ALU.bitwise_and).then_inc(vchain, 1)
                chain[0] += 1
                link(nc.vector.tensor_reduce(amax[:, :], blocks(rows), AXX, ALU.max, apply_absolute_value=True))
                link(nc.vector.tensor_scalar(amax[:, :], amax[:, :], 1e-30, None, ALU.max))
                link(nc.vector.tensor_scalar(amax[:, :].bitcast(U32), amax[:, :].bitcast(U32), 0x7F800000, None,
                                             ALU.bitwise_and))
                link(nc.vector.tensor_scalar(scale_half[:, :], amax[:, :], 0.125, None, ALU.mult))
                link(nc.vector.reciprocal(inv_scale[:, :], amax[:, :]))
                link(nc.vector.tensor_scalar(inv_scale[:, :], inv_scale[:, :], 4.0, None, ALU.mult))
                link(nc.vector.tensor_tensor(blocks(w_abs), blocks(w_abs), wide(inv_scale), ALU.mult))
                link(nc.vector.tensor_scalar(w_acc[:, :], w_abs[:, :], 5.0, 2.0, ALU.is_ge, ALU.mult))
                for mid in (3.5, 2.5):
                    link(nc.vector.scalar_tensor_tensor(w_acc[:, :], w_abs[:, :], mid, w_acc[:, :], ALU.is_ge, ALU.add))
                link(nc.vector.tensor_scalar(w_acc[:, :], w_acc[:, :], 2.0, None, ALU.mult))
                for mid in (1.75, 1.25, 0.75, 0.25):
                    link(nc.vector.scalar_tensor_tensor(w_acc[:, :], w_abs[:, :], mid, w_acc[:, :], ALU.is_ge, ALU.add))
                link(nc.vector.tensor_tensor(blocks(w_acc), blocks(w_acc), wide(scale_half), ALU.mult))
                nc.vector.tensor_scalar(rows[:, :].bitcast(U32), rows[:, :].bitcast(U32), 0x80000000, None,
                                        ALU.bitwise_and).then_inc(vchain, 1)
                chain[0] += 1
                dve.wait_ge(vchain, chain[0])
                nc.vector.tensor_tensor(rows[:, :].bitcast(U32), rows[:, :].bitcast(U32), w_acc[:, :].bitcast(U32),
                                        ALU.bitwise_or).then_inc(quant_ready, 1)
                dve.wait_ge(quant_ready, n + 1)

            statistics(0)
            for b in range(BATCH):
                if b + 1 < BATCH:
                    statistics(b + 1)
                normalise(b)
                low_parts(b)
            quantise(0)
            quantise(1)

            def split_gelu(g, f):
                dve.wait_ge(gelu_ready, g * FT + f + 1)
                if f >= 4 or not isinstance(g, int):
                    dve.wait_ge(down_ready, g * FT + f - 3)
                nc.vector.tensor_copy(g_hi[:, f % 4, :], g_full[:, f % 2, :]).then_inc(g_hi_ready, 1)
                dve.wait_ge(g_hi_ready, g * FT + f + 1)
                nc.vector.tensor_tensor(g_lo[:, f % 4, :], g_full[:, f % 2, :], g_hi[:, f % 4, :].bitcast(F32),
                                        ALU.subtract).then_inc(g_lo_ready, 1)

            def sum_rows(g, s, g2):
                dve.wait_ge(down_ready, g * FT + FT)
                if g2 is not None:
                    dve.wait_ge(y_stored[s], g2 * 16)
                t = 4 * g
                nc.vector.tensor_tensor(y_out[:, s, :, :], y_ps[:, :, 0:DIM], x_all[:, bass.ds(t, 4), :],
                                        ALU.add).then_inc(y_ready, 1)

            dve.wait_ge(xb_ready, TILES)
            for g in range(2):
                for f in range(FT):
                    split_gelu(g, f)
                sum_rows(g, g, None)
            with dve.Fori(1, GROUPS // 2) as g2:
                for s in range(2):
                    g = g2 * 2 + s
                    for f in range(FT):
                        split_gelu(g, f)
                    sum_rows(g, s, g2)

        @block.tensor
        def _(pe):
            pe.wait_ge(small_loaded, 48)
            for b in range(BATCH):
                pe.wait_ge(xn_ready, b + 1)
                for n in range(4):
                    c, h = n // 2, n % 2
                    if 4 * b + n >= 2:
                        pe.wait_ge(xt_lo_ready, 4 * b + n - 1)
                    for i in range(4):
                        last = nc.tensor.transpose(bank[n % 2][:, i * P:(i + 1) * P],
                                                   xn[:, 4 * h + i, c * P:(c + 1) * P], ident[:, :])
                    last.then_inc(xt_ready, 1)
            pe.wait_ge(xt_lo_ready, 4 * BATCH)
            for n in range(8):
                k = n // 4
                pe.wait_ge(quant_ready, k + 1)
                if n >= 2:
                    pe.wait_ge(wt_copied, n - 1)
                for i in range(4):
                    if k == 0:
                        col = (4 * (n % 2) + i) * DIM + (n // 2) * P
                    else:
                        col = (i % 2) * FF + (2 * (n - 4) + i // 2) * P
                    last = nc.tensor.transpose(bank[n % 2][:, i * P:(i + 1) * P], w_rows[k][:, col:col + P], ident[:, :])
                last.then_inc(wt_ready, 1)
            pe.wait_ge(wt_copied, 8)

            def up(g, f, first):
                if not first:
                    pe.wait_ge(gelu_ready, g * FT + f - 1)
                for n in range(2 * CT):
                    c, part = n // 2, (xnt_hi, xnt_lo)[n % 2]
                    last = nc.tensor.matmul(bank[f % 2][:, :], up_w[:, c, f * P:(f + 1) * P],
                                            part[:, c, bass.ds(g * HALF, HALF)], start=(n == 0), stop=(n == 2 * CT - 1))
                last.then_inc(up_ready, 1)

            def down(g, f, first):
                pe.wait_ge(g_lo_ready, g * FT + f + 1)
                if f == 0 and not first:
                    pe.wait_ge(y_ready, g)
                for t in range(4):
                    for n, part in enumerate((g_hi, g_lo)):
                        last = nc.tensor.matmul(y_ps[:, t, 0:DIM], part[:, f % 4, t * P:(t + 1) * P], down_w[:, f, :],
                                                start=(f == 0 and n == 0), stop=(f == FT - 1 and n == 1))
                last.then_inc(down_ready, 1)

            up(0, 0, True)
            up(0, 1, True)
            for f in range(FT):
                up(f // 6, (f + 2) % FT, False)
                down(0, f, True)
            with pe.Fori(1, GROUPS - 1) as g:
                for f in range(FT):
                    up(g + f // 6, (f + 2) % FT, False)
                    down(g, f, False)
            for f in range(FT):
                if f + 2 < FT:
                    up(GROUPS - 1, f + 2, False)
                down(GROUPS - 1, f, False)


def stage_two(nc, d):
    with ExitStack() as ctx:
        def sb(name, shape, dt=F32):
            return ctx.enter_context(nc.sbuf_tensor(name, shape, dt))

        def sem(name):
            return ctx.enter_context(nc.semaphore(name))

        def pb(name, shape):
            return ctx.enter_context(nc.psum_tensor(name, shape, F32))

        ident = sb("ident2", [P, P])
        cos = sb("cos", [P, SEQ])
        sin = sb("sin", [P, SEQ])
        x_hi = sb("x_hi", [P, CT, SEQ], F32R)
        x_lo = sb("x_lo", [P, CT, SEQ], F32R)
        w_raw = sb("w_raw", [P, CT, WCOLS])
        w_hi = sb("w_hi", [P, CT, WCOLS], F32R)
        w_lo = sb("w_lo", [P, CT, WCOLS], F32R)
        wo_raw = sb("wo_raw", [P, 2, DIM])
        wo_hi = sb("wo_hi", [P, 2, DIM], F32R)
        wo_lo = sb("wo_lo", [P, 2, DIM], F32R)
        qk_hi = sb("qk_hi", [P, 2, 2, SEQ], F32R)
        qk_lo = sb("qk_lo", [P, 2, 2, SEQ], F32R)
        v_hi = sb("v_hi", [P, 2, BT, 2 * HEAD], F32R)
        v_lo = sb("v_lo", [P, 2, BT, 2 * HEAD], F32R)
        rope_a = sb("rope_a", [P, 2, HALF])
        rope_b = sb("rope_b", [P, 2, HALF])
        probs = sb("probs", [P, 4, SEQ])
        pt_hi = sb("pt_hi", [P, 2, BT, CHUNK], F32R)
        pt_lo = sb("pt_lo", [P, 2, BT, CHUNK], F32R)
        o_hi = sb("o_hi", [P, 2, CHUNK], F32R)
        o_lo = sb("o_lo", [P, 2, CHUNK], F32R)
        y = sb("y", [P, BT, DIM])
        neg_max = sb("neg_max", [P, 16])
        row_sum = sb("row_sum", [P, 16])
        inv_sum = sb("inv_sum", [P, 16])

        s_ps = [pb(f"s_ps{i}", [P, SEQ]) for i in range(2)]
        t_ps = [pb(f"t_ps{i}", [P, 4, P]) for i in range(2)]
        o_ps = pb("o_ps", [P, 512])
        w_ps = pb("w_ps", [P, 512])

        const_loaded = sem("const_loaded")
        x_loaded = sem("xt_loaded")
        PARTS = {"qk0": slice(0, 256), "qk1": slice(256, 512), "v": slice(512, 768)}
        w_loaded = {k: sem(f"w_loaded_{k}") for k in PARTS}
        w_hi_ready = {k: sem(f"w_hi_{k}") for k in PARTS}
        w_lo_ready = {k: sem(f"w_lo_{k}") for k in PARTS}
        wo_loaded = [sem(f"wo_loaded{i}") for i in range(2)]
        wo_hi_ready = [sem(f"wo_hi{i}") for i in range(2)]
        wo_lo_ready = [sem(f"wo_lo{i}") for i in range(2)]
        proj_ready = sem("proj_ready")
        rope_in = sem("rope_in")
        rope_step = sem("rope_step")
        qk_ready = sem("qk_ready")
        v_hi_ready = sem("v_hi_ready")
        v_lo_ready = sem("v_lo_ready")
        scores_ready = sem("scores_ready")
        max_ready = sem("max_ready")
        probs_ready = sem("probs_ready")
        pt_ready = sem("pt_ready")
        pt_hi_ready = sem("pt_hi_ready")
        pt_lo_ready = sem("pt_lo_ready")
        o_ready = sem("o_ready")
        o_hi_ready = sem("o_hi_ready")
        o_lo_ready = sem("o_lo_ready")
        inv_ready = sem("inv_ready")
        out_ready = sem("out_ready")
        y_added = sem("y_added")
        y_loaded = [sem(f"y_loaded{c}") for c in range(4)]
        y_stored = sem("y_stored2")

        block = ctx.enter_context(nc.Block())

        GROUPS = {(3, 0): (0, "qk0", 0), (3, 1): (1, "qk0", 1), (4, 0): (2, "qk0", 2), (4, 1): (3, "v", 0),
                  (5, 0): (4, "qk0", 3), (5, 1): (5, "v", 1), (6, 0): (6, "v", 2), (6, 1): (7, "v", 3),
                  (7, 0): (8, "qk1", 0), (7, 1): (9, "qk1", 1), (0, 0): (10, "qk1", 2), (1, 0): (11, "qk1", 3)}

        def group_at(k, slot, last):
            g = GROUPS.get((k % 8, slot))
            if g is None:
                return None
            ahead = k // 8 + (1 if k % 8 >= 3 else 0)
            if last and ahead > 1:
                return None
            return (*g, ahead)

        def qk_number(part, n):
            return n + (4 if part == "qk1" else 0)

        PEELED = 4

        def steps(eng, step):
            for k in range(PEELED):
                step(0, k, True, False)
            with eng.Fori(0, PAIRS // 2 - 1) as i:
                for k in range(PEELED, PEELED + 16):
                    if k < 16:
                        step(i, k, False, False)
                    else:
                        step(i + 1, k - 16, False, False)
            for k in range(PEELED, 18):
                step(PAIRS // 2 - 1, k, False, True)

        @block.sync
        def _(sp):
            def load_part(p, pw, part, first=False):
                if not first:
                    sp.wait_ge(w_lo_ready[part], p)
                    sp.wait_ge(w_hi_ready[part], p)
                sp.dma_start(w_raw[:, :, PARTS[part]], d["w_qkv"][pw][:, :, PARTS[part]]).then_inc(w_loaded[part], 16)

            def load_wo(p, pw, h, first=False):
                if not first:
                    sp.wait_ge(wo_lo_ready[h], p)
                    sp.wait_ge(wo_hi_ready[h], p)
                sp.dma_start(wo_raw[:, h, :], d["w_out"][pw][:, h, :]).then_inc(wo_loaded[h], 16)

            def load_x(b):
                cols = slice(b * SEQ, (b + 1) * SEQ) if isinstance(b, int) else bass.ds(b * SEQ, SEQ)
                sp.dma_start(x_hi[:, :, :].bitcast(F32), d["xnt"][0][:, :, cols]).then_inc(x_loaded, 16)
                sp.dma_start(x_lo[:, :, :].bitcast(F32), d["xnt"][1][:, :, cols]).then_inc(x_loaded, 16)

            def load_y(b, c):
                sp.dma_start(y[:, 2 * c:2 * c + 2, :], d["y"][:, bass.ds(b * BT + 2 * c, 2), :]).then_inc(y_loaded[c], 16)

            def store_y(b, c):
                sp.wait_ge(y_added, b * 64 + 61 + c)
                sp.dma_start(d["out"][:, bass.ds(b * BT + 2 * c, 2), :], y[:, 2 * c:2 * c + 2, :]).then_inc(y_stored, 16)

            for part in PARTS:
                load_part(0, 0, part, True)
            load_x(0)
            for name, dst in (("cos", cos), ("sin", sin), ("ident", ident)):
                sp.dma_start(dst[:, :], d[name]).then_inc(const_loaded, 16)
            load_wo(0, 0, 0, True)
            load_wo(0, 0, 1, True)
            for c in range(4):
                load_y(0, c)

            def pair(b, j):
                p = b * PAIRS_PER_SEQ + j
                load_part(p, j, "qk0")
                load_part(p, j, "v")
                load_part(p, j, "qk1")
                load_wo(p, j, 0)
                if j == 0:
                    sp.wait_ge(proj_ready, b * 96)
                    load_x(b)
                if j == 1 and not isinstance(b, int):
                    for c in range(4):
                        store_y(b - 1, c)
                        sp.wait_ge(y_stored, (b - 1) * 64 + 16 * (c + 1))
                        load_y(b, c)
                load_wo(p, j, 1)

            for j in range(1, PAIRS_PER_SEQ):
                pair(0, j)
            with sp.Fori(1, BATCH) as b:
                for j in range(PAIRS_PER_SEQ):
                    pair(b, j)
            for c in range(4):
                store_y(BATCH - 1, c)
            sp.wait_ge(y_stored, 64 * BATCH)

        @block.gpsimd
        def _(pool):
            def w_low(p, part, first=False):
                cols = PARTS[part]
                pool.wait_ge(w_hi_ready[part], p + 1)
                nc.gpsimd.tensor_tensor(w_lo[:, :, cols], w_raw[:, :, cols], w_hi[:, :, cols].bitcast(F32),
                                        ALU.subtract).then_inc(w_lo_ready[part], 1)

            def wo_low(p, h):
                pool.wait_ge(wo_hi_ready[h], p + 1)
                nc.gpsimd.tensor_tensor(wo_lo[:, h, :], wo_raw[:, h, :], wo_hi[:, h, :].bitcast(F32),
                                        ALU.subtract).then_inc(wo_lo_ready[h], 1)

            def rotate(p, part, n):
                m = qk_number(part, n)
                g = p * 8 + m
                slot, kind, half = m % 2, 1 - n // 2, n % 2
                cols = slice(half * HALF, (half + 1) * HALF)
                head = 0 if part == "qk0" else 1
                a, b = rope_a[:, slot, :], rope_b[:, slot, :]
                hi, lo = qk_hi[:, head, kind, cols], qk_lo[:, head, kind, cols]
                pool.wait_ge(rope_in, g + 1)
                nc.gpsimd.tensor_tensor(a, a, cos[:, cols], ALU.mult).then_inc(rope_step, 1)
                nc.gpsimd.tensor_tensor(b, b, sin[:, cols], ALU.mult).then_inc(rope_step, 1)
                pool.wait_ge(rope_step, g * 4 + 2)
                nc.gpsimd.tensor_tensor(hi, a, b, ALU.add).then_inc(rope_step, 1)
                pool.wait_ge(rope_step, g * 4 + 3)
                nc.gpsimd.tensor_tensor(a, a, b, ALU.add).then_inc(rope_step, 1)
                pool.wait_ge(rope_step, g * 4 + 4)
                nc.gpsimd.tensor_tensor(lo, a, hi.bitcast(F32), ALU.subtract).then_inc(qk_ready, 1)

            pool.wait_ge(const_loaded, 48)
            for part in PARTS:
                w_low(0, part)
            for n in range(4):
                rotate(0, "qk0", n)
            wo_low(0, 0)
            rotate(0, "qk1", 0)
            rotate(0, "qk1", 1)

            def step(i, k, first, last):
                k8 = k % 8
                more = not (last and k >= 8)
                p = i * 2 + k // 8
                if k8 == 0 and more:
                    w_low(p + 1, "qk0")
                    w_low(p + 1, "v")
                if k8 == 3:
                    wo_low(p, 1)
                if k8 == 4 and more:
                    w_low(p + 1, "qk1")
                if k8 == 6 and more:
                    wo_low(p + 1, 0)
                for slot in (0, 1):
                    g = group_at(k, slot, last)
                    if g and g[1] != "v":
                        rotate(i * 2 + g[3], g[1], g[2])

            steps(pool, lambda i, k, first, last: None if k >= 16 else step(i, k, first, last))

        @block.scalar
        def _(act):
            def w_high(p, part, first=False):
                cols = PARTS[part]
                act.wait_ge(w_loaded[part], (p + 1) * 16)
                if not first:
                    act.wait_ge(proj_ready, p * 12 - (0 if part == "qk1" else 4))
                nc.scalar.activation(w_hi[:, :, cols], w_raw[:, :, cols], ACT.Copy).then_inc(w_hi_ready[part], 1)

            def wo_high(p, h, first=False):
                act.wait_ge(wo_loaded[h], (p + 1) * 16)
                if not first:
                    act.wait_ge(out_ready, p * 8 - (4 if h == 0 else 0))
                nc.scalar.activation(wo_hi[:, h, :], wo_raw[:, h, :], ACT.Copy).then_inc(wo_hi_ready[h], 1)

            def take_group(p, place, part, n, first=False):
                act.wait_ge(proj_ready, p * 12 + place + 1)
                if part == "v":
                    nc.scalar.activation(v_hi[:, take_group.parity, 2 * n:2 * n + 2, :],
                                         w_ps[:, :].rearrange("p (a b) -> p a b", a=2), ACT.Copy).then_inc(v_hi_ready, 1)
                    return
                m = qk_number(part, n)
                if not (first and m < 2):
                    act.wait_ge(qk_ready, p * 8 + m - 1)
                scale = SCALE if n // 2 == 1 else 1.0
                a, b = rope_a[:, m % 2, :], rope_b[:, m % 2, :]
                h = HEAD // 2
                nc.scalar.activation(a, w_ps[:, :], ACT.Copy, scale=scale)
                nc.scalar.activation(b[0:h], w_ps[h:P, :], ACT.Copy, scale=scale)
                nc.scalar.activation(b[h:P], w_ps[0:h, :], ACT.Copy, scale=scale).then_inc(rope_in, 1)

            def exponentials(t, k2):
                act.wait_ge(max_ready, t + 1)
                nc.scalar.activation(probs[:, k2 % 4, :], s_ps[k2 % 2][:, :], ACT.Exp, bias=neg_max[:, k2 % 16:k2 % 16 + 1],
                                     accum_out=row_sum[:, k2 % 16:k2 % 16 + 1]).then_inc(probs_ready, 1)

            def high_tile(t, k2):
                for h in range(2):
                    act.wait_ge(pt_ready, t * 2 + h + 1)
                    nc.scalar.activation(pt_hi[:, (k2 // 2) % 2, 4 * h:4 * h + 4, (k2 % 2) * P:(k2 % 2 + 1) * P],
                                         t_ps[h][:, :, :], ACT.Copy).then_inc(pt_hi_ready, 1)

            def high_out(c, slot):
                act.wait_ge(o_ready, c + 1)
                nc.scalar.activation(o_hi[:, slot, :], o_ps[:, 0:CHUNK], ACT.Copy).then_inc(o_hi_ready, 1)

            for part in PARTS:
                w_high(0, part, True)
            take_group.parity = 0
            for place, part, n in sorted(GROUPS.values())[:10]:
                take_group(0, place, part, n, True)
            wo_high(0, 0, True)
            exponentials(0, 0)
            exponentials(1, 1)

            def step(i, k, first, last):
                c = i * 16 + k
                t = c * 2
                p = i * 2 + k // 8
                more = not (last and k >= 8)
                tail = last and k >= 16
                if k % 8 == 0 and more and not tail:
                    w_high(p + 1, "qk0")
                    w_high(p + 1, "v")
                if k % 8 == 3:
                    wo_high(p, 1, first or (isinstance(p, int) and p == 0))
                if k % 8 == 4 and more:
                    w_high(p + 1, "qk1")
                if k % 8 == 6 and more:
                    wo_high(p + 1, 0)
                if not (first and k == 0):
                    g = group_at((k - 1) % 16, 1, last) if k > 0 else group_at(15, 1, False)
                    if tail:
                        g = None
                    if g:
                        ahead = g[3] - (2 if k == 0 else 0)
                        take_group.parity = g[3] % 2
                        take_group(i * 2 + ahead, *g[:3])
                if not tail:
                    high_tile(t, 2 * k)
                    g = group_at(k, 0, last)
                    if g:
                        take_group.parity = g[3] % 2
                        take_group(i * 2 + g[3], *g[:3])
                    if not (last and k == 15):
                        exponentials(t + 2, 2 * k + 2)
                    high_tile(t + 1, 2 * k + 1)
                    if not (last and k == 15):
                        exponentials(t + 3, 2 * k + 3)
                if not (first and k == 0) and not (last and k == 17):
                    high_out(c - 1, (k - 1) % 2)

            steps(act, step)

        @block.vector
        def _(dve):
            def v_low(p, n, parity):
                dve.wait_ge(v_hi_ready, p * 4 + n + 1)
                hi = v_hi[:, parity, 2 * n:2 * n + 2, :]
                nc.vector.tensor_tensor(v_lo[:, parity, 2 * n:2 * n + 2, :],
                                        w_ps[:, :].rearrange("p (a b) -> p a b", a=2), hi.bitcast(F32),
                                        ALU.subtract).then_inc(v_lo_ready, 1)

            def row_max(t, k2):
                dve.wait_ge(scores_ready, t + 1)
                nc.vector.tensor_reduce(neg_max[:, k2 % 16:k2 % 16 + 1], s_ps[k2 % 2][:, :], AXX, ALU.max,
                                        negate=True).then_inc(max_ready, 1)

            def low_tile(t, k2):
                for h in range(2):
                    dve.wait_ge(pt_hi_ready, t * 2 + h + 1)
                    at = (slice(None), (k2 // 2) % 2, slice(4 * h, 4 * h + 4), slice((k2 % 2) * P, (k2 % 2 + 1) * P))
                    nc.vector.tensor_tensor(pt_lo[at], t_ps[h][:, :, :], pt_hi[at].bitcast(F32),
                                            ALU.subtract).then_inc(pt_lo_ready, 1)

            def invert(c, k2):
                dve.wait_ge(probs_ready, c * 2 + 2)
                at = slice(k2 % 16, k2 % 16 + 2)
                nc.vector.reciprocal(inv_sum[:, at], row_sum[:, at]).then_inc(inv_ready, 1)

            def low_out(c, slot):
                dve.wait_ge(o_hi_ready, c + 1)
                nc.vector.tensor_tensor(o_lo[:, slot, :], o_ps[:, 0:CHUNK], o_hi[:, slot, :].bitcast(F32),
                                        ALU.subtract).then_inc(o_lo_ready, 1)

            def add_out(c, k, b):
                dve.wait_ge(out_ready, c + 1)
                dve.wait_ge(inv_ready, c + 1)
                dve.wait_ge(y_loaded[k % 4], (b + 1) * 16)
                for n in range(2):
                    col = (2 * k + n) % 16
                    rows = y[:, 2 * (k % 4) + n, :]
                    last = nc.vector.scalar_tensor_tensor(rows, w_ps[:, n * DIM:(n + 1) * DIM], inv_sum[:, col:col + 1],
                                                          rows, ALU.mult, ALU.add)
                last.then_inc(y_added, 1)

            for n in range(4):
                v_low(0, n, 0)
            row_max(0, 0)
            row_max(1, 1)

            def step(i, k, first, last):
                c = i * 16 + k
                t = c * 2
                tail = last and k >= 16
                has_out = not (first and k < 2)
                g = group_at((k - 1) % 16, 1, last) if k > 0 and not tail else None
                if g and g[1] == "v":
                    v_low(i * 2 + g[3], g[2], g[3] % 2)
                if not tail:
                    low_tile(t, 2 * k)
                    if not (last and k == 15):
                        row_max(t + 2, 2 * k + 2)
                if has_out:
                    invert(c - 2, 2 * k - 4)
                if not tail:
                    g = group_at(k, 0, last)
                    if g and g[1] == "v":
                        v_low(i * 2 + g[3], g[2], g[3] % 2)
                    if not (last and k == 15):
                        row_max(t + 3, 2 * k + 3)
                if has_out:
                    b = (i // 4) if k >= 2 else ((i - 1) // 4)
                    add_out(c - 2, (k - 2) % 16, b)
                if not tail:
                    low_tile(t + 1, 2 * k + 1)
                if not (first and k == 0) and not (last and k == 17):
                    low_out(c - 1, (k - 1) % 2)

            steps(dve, step)

        @block.tensor
        def _(pe):
            THREE = lambda hi, lo: ((hi[0], hi[1]), (hi[0], lo[1]), (lo[0], hi[1]))

            def chain(out, terms, inc=None):
                for n, (w, m) in enumerate(terms):
                    ins = nc.tensor.matmul(out, w, m, start=(n == 0), stop=(n == len(terms) - 1))
                if inc is not None:
                    ins.then_inc(inc, 1)

            def project(p, place, part, n, parity):
                if part == "v":
                    for t in range(2):
                        tok = slice((2 * n + t) * P, (2 * n + t + 1) * P)
                        cols = PARTS["v"]
                        chain(w_ps[:, t * 256:(t + 1) * 256],
                              [term for c in range(CT) for term in
                               ((x_hi[:, c, tok], w_hi[:, c, cols]), (x_hi[:, c, tok], w_lo[:, c, cols]),
                                (x_lo[:, c, tok], w_hi[:, c, cols]))],
                              proj_ready if t == 1 else None)
                    return
                kind, half = 1 - n // 2, n % 2
                col = PARTS[part].start + kind * HEAD
                cols, tok = slice(col, col + HEAD), slice(half * HALF, (half + 1) * HALF)
                chain(w_ps[:, :],
                      [term for c in range(CT) for term in
                       ((w_hi[:, c, cols], x_hi[:, c, tok]), (w_hi[:, c, cols], x_lo[:, c, tok]),
                        (w_lo[:, c, cols], x_hi[:, c, tok]))], proj_ready)

            def bank_free(i, k, slot):
                c = i * 16 + k
                before = [(k, s) for s in range(slot)][::-1] + [(k - 1, s) for s in (2, 1, 0)] + [(k - 2, s) for s in (2, 1)]
                for kk, s in before:
                    if s == 1 and bank_free.first and kk < 2:
                        continue
                    if s == 1:
                        pe.wait_ge(y_added, c - (k - kk) - 1)
                        return
                    g = group_at(kk % 16, s // 2, bank_free.last and kk >= 0)
                    if g:
                        ahead = g[3] - (2 if kk < 0 else 0)
                        if g[1] == "v":
                            pe.wait_ge(v_lo_ready, (i * 2 + ahead) * 4 + g[2] + 1)
                        else:
                            pe.wait_ge(rope_in, (i * 2 + ahead) * 8 + qk_number(g[1], g[2]) + 1)
                        return

            def scores(t, k2, head, p, first_tile):
                if first_tile:
                    pe.wait_ge(qk_ready, p * 8 + 4 * (head + 1))
                tile = (k2 % 8) * P
                q_hi, q_lo = qk_hi[:, head, 0, tile:tile + P], qk_lo[:, head, 0, tile:tile + P]
                for h in range(2):
                    keys = slice(h * HALF, (h + 1) * HALF)
                    k_hi, k_lo = qk_hi[:, head, 1, keys], qk_lo[:, head, 1, keys]
                    chain(s_ps[k2 % 2][:, keys], ((q_hi, k_hi), (q_hi, k_lo), (q_lo, k_hi)),
                          scores_ready if h == 1 else None)

            def turn(t, k2, first):
                pe.wait_ge(probs_ready, t + 1)
                for h in range(2):
                    if not first:
                        pe.wait_ge(pt_lo_ready, t * 2 + h - 1)
                    for j in range(4):
                        kt = 4 * h + j
                        ins = nc.tensor.transpose(t_ps[h][:, j, :], probs[:, k2 % 4, kt * P:(kt + 1) * P], ident[:, :])
                    ins.then_inc(pt_ready, 1)

            def values(c, k, p, first):
                pe.wait_ge(pt_lo_ready, c * 4 + 4)
                if not first:
                    pe.wait_ge(o_lo_ready, c)
                if k % 8 == 0:
                    pe.wait_ge(v_lo_ready, p * 4 + 4)
                parity, head, slot = (k // 8) % 2, (k // 4) % 2, k % 2
                cols = slice(head * HEAD, (head + 1) * HEAD)
                chain(o_ps[:, 0:CHUNK],
                      [term for kt in range(BT) for term in
                       ((v_hi[:, parity, kt, cols], pt_hi[:, slot, kt, :]), (v_hi[:, parity, kt, cols], pt_lo[:, slot, kt, :]),
                        (v_lo[:, parity, kt, cols], pt_hi[:, slot, kt, :]))], o_ready)

            def output(c, k, p):
                head, slot = (k // 4) % 2, k % 2
                pe.wait_ge(o_lo_ready, c + 1)
                if k % 4 == 0:
                    pe.wait_ge(wo_lo_ready[head], p + 1)
                for n in range(2):
                    rows = slice(n * P, (n + 1) * P)
                    chain(w_ps[:, n * DIM:(n + 1) * DIM],
                          ((o_hi[:, slot, rows], wo_hi[:, head, :]), (o_hi[:, slot, rows], wo_lo[:, head, :]),
                           (o_lo[:, slot, rows], wo_hi[:, head, :])), out_ready if n == 1 else None)

            pe.wait_ge(x_loaded, 32)
            pe.wait_ge(const_loaded, 48)
            order = sorted(GROUPS.values())[:10]
            for place, part, n in order:
                pe.wait_ge(w_lo_ready[part], 1)
                if place:
                    _, last_part, last_n = order[place - 1]
                    if last_part == "v":
                        pe.wait_ge(v_lo_ready, last_n + 1)
                    else:
                        pe.wait_ge(rope_in, qk_number(last_part, last_n) + 1)
                project(0, place, part, n, 0)
            scores(0, 0, 0, 0, True)
            scores(1, 1, 0, 0, False)

            def step(i, k, first, last):
                c = i * 16 + k
                t = c * 2
                tail = last and k >= 16
                bank_free.first, bank_free.last = first, last

                def next_scores(n):
                    if last and k == 15:
                        return
                    k2 = 2 * k + 2 + n
                    scores(t + 2 + n, k2, (k2 // 8) % 2, i * 2 + k2 // 16, k2 % 8 == 0)

                def group(slot):
                    g = group_at(k, slot, last)
                    if not g:
                        return
                    place, part, n, ahead = g
                    pn = i * 2 + ahead
                    if not (first and k == 0 and slot == 0):
                        bank_free(i, k, 2 * slot)
                    else:
                        pe.wait_ge(rope_in, 6)
                    if n == 0:
                        pe.wait_ge(w_lo_ready[part], pn + 1)
                    if place == 0:
                        b = i // 4 if ahead == 1 else (i + 1) // 4
                        pe.wait_ge(x_loaded, (b + 1) * 32)
                    project(pn, place, part, n, ahead % 2)

                if not tail:
                    turn(t, 2 * k, first and k == 0)
                    next_scores(0)
                    group(0)
                    turn(t + 1, 2 * k + 1, False)
                    next_scores(1)
                if not (first and k < 2):
                    bank_free(i, k, 1)
                    output(c - 2, (k - 2) % 16, i * 2 + (k - 2) // 8)
                if not (first and k == 0) and not (last and k == 17):
                    values(c - 1, (k - 1) % 16, i * 2 + (k - 1) // 8, first and k == 1)
                if not tail:
                    group(1)

            steps(pe, step)


def _rope_tables():
    inv = (np.float32(1.0) / np.power(np.float32(10000.0), np.arange(0, HEAD, 2, dtype=np.float32) / np.float32(HEAD))).astype(np.float32)
    angle = (np.arange(SEQ, dtype=np.float32)[None, :] * inv[:, None]).astype(np.float32)
    cos, sin = np.cos(angle.astype(np.float64)), np.sin(angle.astype(np.float64))
    return np.concatenate([cos, cos]).astype(np.float32), np.concatenate([-sin, sin]).astype(np.float32)


def build(nc, ins, outs):
    d = dict(ins)
    d["xnt"] = nc.dram_tensor("xnt_parts", [2, P, CT, TOK], F32, kind="Internal").ap()
    d["y"] = nc.dram_tensor("x_plus_ffn", [P, TILES, DIM], F32, kind="Internal").ap()
    d["out"] = outs["out"].rearrange("(t p) c -> p t c", p=P)
    d["x"] = [ins["x"][b * SEQ:(b + 1) * SEQ, :].rearrange("(t p) c -> p t c", p=P) for b in range(BATCH)]
    stage_one(nc, d)
    stage_two(nc, d)


def kernel(L0_attn_x, L0_attn_w_qkv, L0_attn_w_out, L0_ffn_up_kernel, L0_ffn_up_bias, L0_ffn_down_kernel, L0_ffn_down_bias):
    import concourse.bacc as bacc
    from concourse.bass_utils import run_bass_kernel_spmd

    A = np.ascontiguousarray
    cos, sin = _rope_tables()
    w = np.asarray(L0_attn_w_qkv).reshape(3, HEADS // 2, 2, HEAD, CT, P)
    cols = [w[0, :, 0], w[1, :, 0], w[0, :, 1], w[1, :, 1], w[2, :, 0], w[2, :, 1]]
    w_qkv = np.concatenate(cols, axis=1).transpose(0, 3, 2, 1)
    w_out = np.asarray(L0_attn_w_out).reshape(DIM, HEADS // 2, 2, HEAD).transpose(1, 3, 2, 0)
    arrays = {
        "x": A(np.asarray(L0_attn_x).reshape(TOK, DIM)),
        "w_qkv": A(w_qkv),
        "w_out": A(w_out),
        "up_rows": A(np.asarray(L0_ffn_up_kernel).T.reshape(FT, P, DIM).transpose(1, 0, 2).reshape(P, FT * DIM)),
        "down_rows": A(np.asarray(L0_ffn_down_kernel).T.reshape(CT, P, FF).transpose(1, 0, 2).reshape(P, CT * FF)),
        "up_bias": A(np.asarray(L0_ffn_up_bias).reshape(FT, P).T),
        "down_bias": A(np.asarray(L0_ffn_down_bias).reshape(1, DIM)),
        "cos": cos, "sin": sin, "ident": np.eye(P, dtype=np.float32),
    }
    nc = bacc.Bacc("TRN2", target_bir_lowering=False, num_devices=1)
    ins = {n: nc.dram_tensor(f"in_{n}", a.shape, mybir.dt.from_np(a.dtype), kind="ExternalInput").ap() for n, a in arrays.items()}
    outs = {"out": nc.dram_tensor("out_dram", (TOK, DIM), F32, kind="ExternalOutput").ap()}
    build(nc, ins, outs)
    r = run_bass_kernel_spmd(nc, [{f"in_{n}": a for n, a in arrays.items()}], core_ids=[0])
    return r.results[0]["out_dram"].reshape(BATCH, SEQ, DIM)
```

```python
import math
from contextlib import ExitStack

import numpy as np

import concourse.bass as bass
from concourse import mybir

F32 = mybir.dt.float32
F32R = mybir.dt.float32r
U32 = mybir.dt.uint32
ACT = mybir.ActivationFunctionType
ALU = mybir.AluOpType
AXX = mybir.AxisListType.X

BATCH, SEQ, DIM = 4, 1024, 256
HEADS, HEAD = 16, 128
FF = 1024
P = 128
TOK = BATCH * SEQ
TILES = TOK // P
BT = SEQ // P
CT = DIM // P
FT = FF // P
BLOCK = 32
SCALE = 1.0 / math.sqrt(HEAD)
EPS = 1e-5
HALF = SEQ // 2
PAIRS = BATCH * HEADS // 2
PAIRS_PER_SEQ = HEADS // 2
CHUNK = 2 * P
WCOLS = 6 * HEAD
MX_COLS = 2 * DIM * FF // P
MX_STEP = MX_COLS // (PAIRS // 2)
LN_STEP = TILES // (PAIRS // 2)


def layer(nc, d):
    with ExitStack() as ctx:
        def sb(name, shape, dt=F32):
            return ctx.enter_context(nc.sbuf_tensor(name, shape, dt))

        def sem(name):
            return ctx.enter_context(nc.semaphore(name))

        def pb(name, shape):
            return ctx.enter_context(nc.psum_tensor(name, shape, F32))

        ident = sb("ident", [P, P])
        cos = sb("cos", [P, SEQ])
        sin = sb("sin", [P, SEQ])
        seq_parts = sb("seq_parts", [P, BATCH, 2, CT, SEQ], F32R)
        x_hi, x_lo = seq_parts[:, 0, 0], seq_parts[:, 0, 1]
        w_raw = sb("w_raw", [P, CT, WCOLS])
        w_parts = sb("w_parts", [P, 2, CT, WCOLS], F32R)
        w_hi, w_lo = w_parts[:, 0], w_parts[:, 1]
        wo_raw = sb("wo_raw", [P, 2, DIM])
        wo_hi = sb("wo_hi", [P, 2, DIM], F32R)
        wo_lo = sb("wo_lo", [P, 2, DIM], F32R)
        qk_hi, qk_lo = seq_parts[:, 1], seq_parts[:, 2]
        v_hi = seq_parts[:, 3].rearrange("p a c (t n) -> p a (c t) n", n=2 * HEAD)
        v_lo = sb("v_lo", [P, 2, BT, 2 * HEAD], F32R)
        rope_a = sb("rope_a", [P, 2, HALF])
        rope_b = sb("rope_b", [P, 2, HALF])
        probs = sb("probs", [P, 4, SEQ])
        pt_hi = sb("pt_hi", [P, 2, BT, CHUNK], F32R)
        pt_lo = sb("pt_lo", [P, 2, BT, CHUNK], F32R)
        o_hi = sb("o_hi", [P, 2, CHUNK], F32R)
        o_lo = sb("o_lo", [P, 2, CHUNK], F32R)
        y = sb("y", [P, BT, DIM])
        neg_max = sb("neg_max", [P, 16])
        row_sum = sb("row_sum", [P, 16])
        inv_sum = sb("inv_sum", [P, 16])
        ln_x = sb("ln_x", [P, LN_STEP, DIM])
        ln_xn = sb("ln_xn", [P, LN_STEP, DIM])
        ln_hi = sb("ln_hi", [P, CT, LN_STEP * P], F32R)
        ln_lo = sb("ln_lo", [P, CT, LN_STEP * P], F32R)
        ln_mean = sb("ln_mean", [P, BT])
        ln_sq = sb("ln_sq", [P, BT])
        ln_var = sb("ln_var", [P, BT])
        ln_guess = sb("ln_guess", [P, BT])
        ln_step = sb("ln_step", [P, BT])
        ln_rstd = sb("ln_rstd", [P, BT])
        minus_half = sb("minus_half", [P, BT])
        mx_raw = sb("mx_raw", [P, MX_STEP])
        mx_abs = sb("mx_abs", [P, MX_STEP])
        mx_q = sb("mx_q", [P, MX_STEP])
        mx_amax = sb("mx_amax", [P, MX_STEP // BLOCK])
        mx_half = sb("mx_half", [P, MX_STEP // BLOCK])
        mx_inv = sb("mx_inv", [P, MX_STEP // BLOCK])
        mx_turned = sb("mx_turned", [P, MX_STEP])

        up_w = sb("up_w", [P, MX_COLS // 2], F32R)
        down_w = w_parts[:, :, :, :].rearrange("p a b c -> p (a b c)")[:, 0:MX_COLS // 2]
        g_full = probs[:, 0, :].rearrange("p (a b) -> p a b", a=2)
        g_hi, g_lo = (t[:, 0].rearrange("p (f a) c -> p f (a c)", f=4) for t in (pt_hi, pt_lo))
        y_in = probs[:, 1:3, :].rearrange("p s (t c) -> p s t c", c=DIM)
        y_out = y[:, :, :].rearrange("p (s t) c -> p s t c", s=2)
        up_bias = sb("up_bias", [P, FT])
        down_bias = sb("down_bias", [P, DIM])

        s_ps = [pb(f"s_ps{i}", [P, SEQ]) for i in range(2)]
        turn_ps = pb("turn_ps", [P, 2, 4, P])
        t_ps = [turn_ps[:, 0], turn_ps[:, 1]]
        up_ps = [s_ps[0][:, 0:HALF], s_ps[0][:, HALF:SEQ]]
        y_ps = [s_ps[1][:, :].rearrange("p (t c) -> p t c", c=DIM),
                turn_ps[:, :, :, :].rearrange("p a b c -> p (a b c)").rearrange("p (t c) -> p t c", c=DIM)]
        o_ps = pb("o_ps", [P, 512])
        w_ps = pb("w_ps", [P, 512])
        flat = lambda a: a[:, :, :].rearrange("p a b -> p (a b)")
        FIRST_BANKS = [w_ps[:, :], o_ps[:, :], s_ps[1][:, 0:512], s_ps[1][:, 512:1024], flat(t_ps[0]), flat(t_ps[1]),
                       w_ps[:, :], o_ps[:, :], flat(t_ps[0]), flat(t_ps[1])]

        const_loaded = sem("const_loaded")
        ident_loaded = sem("ident_loaded")
        x_ready = sem("x_ready")
        PARTS = {"qk0": slice(0, 256), "qk1": slice(256, 512), "v": slice(512, 768)}
        w_loaded = {k: sem(f"w_loaded_{k}") for k in PARTS}
        w_hi_ready = {k: sem(f"w_hi_{k}") for k in PARTS}
        w_lo_ready = {k: sem(f"w_lo_{k}") for k in PARTS}
        wo_loaded = [sem(f"wo_loaded{i}") for i in range(2)]
        wo_hi_ready = [sem(f"wo_hi{i}") for i in range(2)]
        wo_lo_ready = [sem(f"wo_lo{i}") for i in range(2)]
        proj_ready = sem("proj_ready")
        rope_in = sem("rope_in")
        rope_step = sem("rope_step")
        qk_ready = sem("qk_ready")
        v_hi_ready = sem("v_hi_ready")
        v_lo_ready = sem("v_lo_ready")
        scores_ready = sem("scores_ready")
        max_ready = sem("max_ready")
        probs_ready = sem("probs_ready")
        pt_ready = sem("pt_ready")
        pt_hi_ready = sem("pt_hi_ready")
        pt_lo_ready = sem("pt_lo_ready")
        o_ready = sem("o_ready")
        o_hi_ready = sem("o_hi_ready")
        o_lo_ready = sem("o_lo_ready")
        inv_ready = sem("inv_ready")
        out_ready = sem("out_ready")
        y_added = sem("y_added")
        y_loaded = [sem(f"y_loaded{c}") for c in range(4)]
        y_stored = sem("y_stored")
        ln_loaded = sem("ln_loaded")
        ln_mean_ready = sem("ln_mean_ready")
        ln_sq_ready = sem("ln_sq_ready")
        ln_var_ready = sem("ln_var_ready")
        ln_guess_ready = sem("ln_guess_ready")
        ln_xn_ready = sem("ln_xn_ready")
        ln_turned = sem("ln_turned")
        ln_hi_ready = sem("ln_hi_ready")
        ln_lo_ready = sem("ln_lo_ready")
        ln_stored = sem("ln_stored")
        half_ready = sem("half_ready")
        first_turned = sem("first_turned")
        first_hi = sem("first_hi")
        ln_link = sem("ln_link")
        mx_loaded = sem("mx_loaded")
        mx_link = sem("mx_link")
        mx_ready = sem("mx_ready")
        mx_turned_ready = sem("mx_turned_ready")
        mx_copied = sem("mx_copied")
        mx_stored = sem("mx_stored")
        mx_w_loaded = [sem("up_w_loaded"), sem("down_w_loaded")]
        bias_loaded = sem("bias_loaded")
        seq_loaded = [None] + [sem(f"seq_loaded{b}") for b in range(1, BATCH)]
        y_in_loaded = [sem(f"y_in_loaded{n}") for n in range(2)]
        y_biased = sem("y_biased")
        up_ready = sem("up_ready")
        gelu_ready = sem("gelu_ready")
        g_hi_ready = sem("g_hi_ready")
        g_lo_ready = sem("g_lo_ready")
        down_ready = sem("down_ready")
        rows_ready = sem("rows_ready")
        out_stored = [sem(f"out_stored{n}") for n in range(2)]

        block = ctx.enter_context(nc.Block())

        GROUPS = {(3, 0): (0, "qk0", 0), (3, 1): (1, "qk0", 1), (4, 0): (2, "qk0", 2), (4, 1): (3, "v", 0),
                  (5, 0): (4, "qk0", 3), (5, 1): (5, "v", 1), (6, 0): (6, "v", 2), (6, 1): (7, "v", 3),
                  (7, 0): (8, "qk1", 0), (7, 1): (9, "qk1", 1), (0, 0): (10, "qk1", 2), (1, 0): (11, "qk1", 3)}
        FIRST_GROUPS = sorted(GROUPS.values())[:10]
        LN_SLOT, MX_SLOT = (2, 1), (10, 1)

        MX_PARTS = (2, 3, 4, 5, 6, 7, 8, 9)

        def group_at(k, slot, last):
            g = GROUPS.get((k % 8, slot))
            if g is None:
                return None
            ahead = k // 8 + (1 if k % 8 >= 3 else 0)
            if last and ahead > 1:
                return None
            return (*g, ahead)

        def qk_number(part, n):
            return n + (4 if part == "qk1" else 0)

        def qk_slot(part, n):
            return (0 if part == "qk0" else 1), 1 - n // 2, n % 2

        PEELED = 4
        ROUNDS = PAIRS // 2

        def steps(eng, step):
            for k in range(PEELED):
                step(0, k, True, False)
            with eng.Fori(0, ROUNDS - 1) as i:
                for k in range(PEELED, PEELED + 16):
                    if k < 16:
                        step(i, k, False, False)
                    else:
                        step(i + 1, k - 16, False, False)
            for k in range(PEELED, 18):
                step(ROUNDS - 1, k, False, True)

        GROUPS_FF = TOK // HALF
        GT = HALF // P

        def ln_tile(i):
            return (i * LN_STEP + BT) % TILES

        @block.sync
        def _(sp):
            def load_part(p, pw, part, first=False):
                if not first:
                    sp.wait_ge(w_lo_ready[part], p)
                    sp.wait_ge(w_hi_ready[part], p)
                sp.dma_start(w_raw[:, :, PARTS[part]], d["w_qkv"][pw][:, :, PARTS[part]]).then_inc(w_loaded[part], 16)

            def load_wo(p, pw, h, first=False):
                if not first:
                    sp.wait_ge(wo_lo_ready[h], p)
                    sp.wait_ge(wo_hi_ready[h], p)
                sp.dma_start(wo_raw[:, h, :], d["w_out"][pw][:, h, :]).then_inc(wo_loaded[h], 16)

            def load_x(b):
                cols = bass.ds(b * SEQ, SEQ)
                sp.dma_start(x_hi[:, :, :].bitcast(F32), d["xnt"][0][:, :, cols]).then_inc(x_ready, 16)
                sp.dma_start(x_lo[:, :, :].bitcast(F32), d["xnt"][1][:, :, cols]).then_inc(x_ready, 16)

            def load_y(b, c):
                sp.dma_start(y[:, 2 * c:2 * c + 2, :], d["x"][:, bass.ds(b * BT + 2 * c, 2), :]).then_inc(y_loaded[c], 16)

            def store_y(b, c):
                sp.wait_ge(y_added, b * 64 + 61 + c)
                sp.dma_start(d["y"][:, bass.ds(b * BT + 2 * c, 2), :], y[:, 2 * c:2 * c + 2, :]).then_inc(y_stored, 16)

            def load_ln(i):
                sp.dma_start(ln_x[:, :, :], d["x"][:, bass.ds(ln_tile(i), LN_STEP), :]).then_inc(ln_loaded, 16)

            def load_mx(i):
                sp.dma_start(mx_raw[:, :], d["mx_rows"][:, bass.ds(i * MX_STEP, MX_STEP)]).then_inc(mx_loaded, 16)

            def store_ln(i):
                sp.wait_ge(ln_lo_ready, i + 1)
                tok = bass.ds(ln_tile(i) * P, LN_STEP * P)
                sp.dma_start(d["xnt"][0][:, :, tok], ln_hi[:, :, :].bitcast(F32)).then_inc(ln_stored, 16)
                sp.dma_start(d["xnt"][1][:, :, tok], ln_lo[:, :, :].bitcast(F32)).then_inc(ln_stored, 16)

            def store_mx(i):
                sp.wait_ge(mx_copied, i + 1)
                sp.dma_start(d["mx"][:, bass.ds(i * MX_STEP, MX_STEP)], mx_turned[:, :]).then_inc(mx_stored, 16)

            for c in range(4):
                load_y(0, c)
            load_part(0, 0, "qk0", True)
            sp.dma_start(ident[:, :], d["ident"]).then_inc(ident_loaded, 16)
            load_part(0, 0, "v", True)
            for name, dst in (("cos", cos), ("sin", sin)):
                sp.dma_start(dst[:, :], d[name]).then_inc(const_loaded, 16)
            load_part(0, 0, "qk1", True)
            load_wo(0, 0, 0, True)
            load_wo(0, 0, 1, True)
            load_ln(0)
            load_mx(0)

            def pair(b, j):
                p = b * PAIRS_PER_SEQ + j
                load_part(p, j, "qk0")
                load_part(p, j, "v")
                load_part(p, j, "qk1")
                rounds = b * (PAIRS_PER_SEQ // 2) + j // 2
                if j % 2 == 0:
                    store_ln(rounds - 1)
                    load_ln(rounds)
                elif not isinstance(b, int) or j > 1:
                    store_mx(rounds - 1)
                    load_mx(rounds)
                if j == 0:
                    sp.wait_ge(ln_stored, b * 128)
                load_wo(p, j, 0)
                if j == 0:
                    sp.wait_ge(proj_ready, b * 96)
                    load_x(b)
                if j == 1 and not isinstance(b, int):
                    for c in range(4):
                        store_y(b - 1, c)
                        sp.wait_ge(y_stored, (b - 1) * 64 + 16 * (c + 1))
                        load_y(b, c)
                load_wo(p, j, 1)

            for j in range(1, PAIRS_PER_SEQ):
                pair(0, j)
            with sp.Fori(1, BATCH) as b:
                for j in range(PAIRS_PER_SEQ):
                    pair(b, j)
            store_ln(ROUNDS - 1)
            store_mx(ROUNDS - 1)

            def load_seq(b):
                for part in range(2):
                    sp.dma_start(seq_parts[:, b, part].bitcast(F32),
                                 d["xnt"][part][:, :, b * SEQ:(b + 1) * SEQ]).then_inc(seq_loaded[b], 16)

            def load_rows(g, n):
                sp.dma_start(y_in[:, n], d["y"][:, bass.ds(g * GT, GT), :]).then_inc(y_in_loaded[n], 16)

            def store_rows(g, n):
                sp.wait_ge(rows_ready, (g + 1) * 2)
                sp.dma_start(d["out"][:, bass.ds(g * GT, GT), :], y_out[:, n]).then_inc(out_stored[n], 16)

            sp.dma_start(up_bias[:, :], d["up_bias"]).then_inc(bias_loaded, 16)
            sp.dma_start(down_bias[:, :], d["down_bias"].to_broadcast([P, DIM])).then_inc(bias_loaded, 16)
            sp.wait_ge(proj_ready, PAIRS * 12)
            sp.wait_ge(ln_stored, ROUNDS * 32)
            load_x(0)
            sp.wait_ge(mx_stored, ROUNDS * 16)
            for n in range(2):
                cols = slice(n * MX_COLS // 2, (n + 1) * MX_COLS // 2)
                dst = (up_w[:, :], down_w)[n]
                sp.dma_start(dst.bitcast(F32), d["mx"][:, cols]).then_inc(mx_w_loaded[n], 16)
            sp.wait_ge(scores_ready, TOK * HEADS // P)
            sp.wait_ge(pt_ready, TOK * HEADS // P * 2 - 2)
            for n in range(2):
                load_rows(n, n)
            load_seq(1)
            load_seq(2)
            sp.wait_ge(o_ready, PAIRS * 8)
            load_seq(3)
            for c in range(4):
                store_y(BATCH - 1, c)
            sp.wait_ge(y_stored, 64 * BATCH)
            with sp.Fori(0, GROUPS_FF // 2 - 1) as b:
                for n in range(2):
                    store_rows(b * 2 + n, n)
                    load_rows(b * 2 + n + 2, n)
            for n in range(2):
                store_rows(GROUPS_FF - 2 + n, n)
            for n in range(2):
                sp.wait_ge(out_stored[n], 16 * (GROUPS_FF // 2))

        def rotate(eng, engine, p, part, n):
            m = qk_number(part, n)
            g = p * 8 + m
            head, kind, half = qk_slot(part, n)
            cols = slice(half * HALF, (half + 1) * HALF)
            a, b = rope_a[:, m % 2, :], rope_b[:, m % 2, :]
            hi, lo = qk_hi[:, head, kind, cols], qk_lo[:, head, kind, cols]
            eng.wait_ge(rope_in, g + 1)
            engine.tensor_tensor(a, a, cos[:, cols], ALU.mult).then_inc(rope_step, 1)
            engine.tensor_tensor(b, b, sin[:, cols], ALU.mult).then_inc(rope_step, 1)
            eng.wait_ge(rope_step, g * 4 + 2)
            engine.tensor_tensor(hi, a, b, ALU.add).then_inc(rope_step, 1)
            eng.wait_ge(rope_step, g * 4 + 3)
            engine.tensor_tensor(a, a, b, ALU.add).then_inc(rope_step, 1)
            eng.wait_ge(rope_step, g * 4 + 4)
            engine.tensor_tensor(lo, a, hi.bitcast(F32), ALU.subtract).then_inc(qk_ready, 1)

        @block.gpsimd
        def _(pool):
            def w_low(p, part):
                cols = PARTS[part]
                pool.wait_ge(w_hi_ready[part], p + 1)
                nc.gpsimd.tensor_tensor(w_lo[:, :, cols], w_raw[:, :, cols], w_hi[:, :, cols].bitcast(F32),
                                        ALU.subtract).then_inc(w_lo_ready[part], 1)

            def wo_low(p, h):
                pool.wait_ge(wo_hi_ready[h], p + 1)
                nc.gpsimd.tensor_tensor(wo_lo[:, h, :], wo_raw[:, h, :], wo_hi[:, h, :].bitcast(F32),
                                        ALU.subtract).then_inc(wo_lo_ready[h], 1)

            def guess(n, tiles):
                pool.wait_ge(ln_var_ready, n + 1)
                nc.gpsimd.tensor_tensor(ln_guess[:, 0:tiles], ln_var[:, 0:tiles], minus_half[:, 0:tiles],
                                        ALU.pow).then_inc(ln_guess_ready, 1)

            nc.gpsimd.memset(minus_half[:, :], -0.5).then_inc(half_ready, 1)
            pool.wait_ge(half_ready, 1)
            w_low(0, "qk0")
            guess(0, BT)
            w_low(0, "v")
            w_low(0, "qk1")
            wo_low(0, 0)
            pool.wait_ge(const_loaded, 32)
            pool.wait_ge(qk_ready, 4)
            rotate(pool, nc.gpsimd, 0, "qk1", 0)
            rotate(pool, nc.gpsimd, 0, "qk1", 1)

            def step(i, k, first, last):
                if k >= 16:
                    return
                k8 = k % 8
                more = not (last and k >= 8)
                p = i * 2 + k // 8
                if k8 == 0 and more:
                    w_low(p + 1, "qk0")
                    w_low(p + 1, "v")
                if k8 == 3:
                    wo_low(p, 1)
                if k8 == 4 and more:
                    w_low(p + 1, "qk1")
                if k8 == 6 and more:
                    wo_low(p + 1, 0)
                if k == 1:
                    guess(i + 1, LN_STEP)
                for slot in (0, 1):
                    g = group_at(k, slot, last)
                    if g and g[1] != "v":
                        rotate(pool, nc.gpsimd, i * 2 + g[3], g[1], g[2])

            steps(pool, step)

            pool.wait_ge(bias_loaded, 32)
            with pool.Fori(0, GROUPS_FF // 2) as b:
                for n in range(2):
                    pool.wait_ge(y_in_loaded[n], (b + 1) * 16)
                    for t in range(GT):
                        ins = nc.gpsimd.tensor_tensor(y_in[:, n, t], y_in[:, n, t], down_bias[:, :], ALU.add)
                    ins.then_inc(y_biased, 1)

        @block.scalar
        def _(act):
            def w_high(p, part, first=False):
                cols = PARTS[part]
                act.wait_ge(w_loaded[part], (p + 1) * 16)
                if not first:
                    act.wait_ge(proj_ready, p * 12 - (0 if part == "qk1" else 4))
                nc.scalar.activation(w_hi[:, :, cols], w_raw[:, :, cols], ACT.Copy).then_inc(w_hi_ready[part], 1)

            def wo_high(p, h, first=False):
                act.wait_ge(wo_loaded[h], (p + 1) * 16)
                if not first:
                    act.wait_ge(out_ready, p * 8 - (4 if h == 0 else 0))
                nc.scalar.activation(wo_hi[:, h, :], wo_raw[:, h, :], ACT.Copy).then_inc(wo_hi_ready[h], 1)

            def take_group(p, place, part, n, parity, bank, first=False):
                act.wait_ge(proj_ready, p * 12 + place + 1)
                if part == "v":
                    nc.scalar.activation(v_hi[:, parity, 2 * n:2 * n + 2, :], bank.rearrange("p (a b) -> p a b", a=2),
                                         ACT.Copy).then_inc(v_hi_ready, 1)
                    return
                m = qk_number(part, n)
                if not (first and m < 2):
                    act.wait_ge(qk_ready, p * 8 + m - 1)
                scale = SCALE if n // 2 == 1 else 1.0
                a, b = rope_a[:, m % 2, :], rope_b[:, m % 2, :]
                h = HEAD // 2
                nc.scalar.activation(a, bank, ACT.Copy, scale=scale)
                nc.scalar.activation(b[0:h], bank[h:P], ACT.Copy, scale=scale)
                nc.scalar.activation(b[h:P], bank[0:h], ACT.Copy, scale=scale).then_inc(rope_in, 1)

            def exponentials(t, k2):
                act.wait_ge(max_ready, t + 1)
                col = k2 % 16
                nc.scalar.activation(probs[:, k2 % 4, :], s_ps[k2 % 2][:, :], ACT.Exp, bias=neg_max[:, col:col + 1],
                                     accum_out=row_sum[:, col:col + 1]).then_inc(probs_ready, 1)

            def high_tile(t, k2):
                for h in range(2):
                    act.wait_ge(pt_ready, t * 2 + h + 1)
                    nc.scalar.activation(pt_hi[:, (k2 // 2) % 2, 4 * h:4 * h + 4, (k2 % 2) * P:(k2 % 2 + 1) * P],
                                         t_ps[h][:, :, :], ACT.Copy).then_inc(pt_hi_ready, 1)

            def high_out(c, slot):
                act.wait_ge(o_ready, c + 1)
                nc.scalar.activation(o_hi[:, slot, :], o_ps[:, 0:CHUNK], ACT.Copy).then_inc(o_hi_ready, 1)

            def squares(n, x, tiles, before):
                act.wait_ge(ln_mean_ready, n + 1)
                for t in range(tiles):
                    ins = nc.scalar.activation(ln_xn[:, t % LN_STEP, :], x[:, t, :], ACT.Square, bias=ln_mean[:, t:t + 1],
                                               accum_out=ln_sq[:, t:t + 1])
                    ins.then_inc(ln_sq_ready, 1)
                    if t + LN_STEP < tiles:
                        act.wait_ge(ln_sq_ready, before + t + 1)

            w_high(0, "qk0", True)
            squares(0, y, BT, 0)
            w_high(0, "v", True)
            for n in range(4):
                act.wait_ge(first_turned, n + 1)
                nc.scalar.activation(x_hi[:, n // 2, (n % 2) * HALF:(n % 2 + 1) * HALF],
                                     s_ps[n // 2][:, (n % 2) * HALF:(n % 2 + 1) * HALF], ACT.Copy).then_inc(first_hi, 1)
            w_high(0, "qk1", True)
            wo_high(0, 0, True)
            for (place, part, n), bank in zip(FIRST_GROUPS, FIRST_BANKS):
                take_group(0, place, part, n, 0, bank, True)
            exponentials(0, 0)
            exponentials(1, 1)

            def step(i, k, first, last):
                c = i * 16 + k
                t = c * 2
                p = i * 2 + k // 8
                more = not (last and k >= 8)
                tail = last and k >= 16
                if k % 8 == 0 and more and not tail:
                    w_high(p + 1, "qk0")
                    w_high(p + 1, "v")
                if k % 8 == 3:
                    wo_high(p, 1, first)
                if k % 8 == 4 and more:
                    w_high(p + 1, "qk1")
                if k % 8 == 6 and more:
                    wo_high(p + 1, 0)
                g = None if tail or (first and k == 0) else group_at(k - 1, 1, last)
                if g:
                    take_group(i * 2 + g[3], *g[:3], g[3] % 2, w_ps[:, :])
                if (k - 1, 1) == LN_SLOT:
                    act.wait_ge(ln_turned, i + 1)
                    nc.scalar.activation(ln_hi[:, :, :], w_ps[:, :].rearrange("p (a b) -> p a b", a=CT),
                                         ACT.Copy).then_inc(ln_hi_ready, 1)
                if (k - 1, 1) == MX_SLOT:
                    act.wait_ge(mx_turned_ready, i + 1)
                    nc.scalar.activation(mx_turned[:, :], w_ps[:, 0:MX_STEP], ACT.Copy).then_inc(mx_copied, 1)
                if not tail:
                    high_tile(t, 2 * k)
                    if k == 1:
                        squares(i + 1, ln_x, LN_STEP, 0)
                    g = group_at(k, 0, last)
                    if g:
                        take_group(i * 2 + g[3], *g[:3], g[3] % 2, w_ps[:, :])
                    if not (last and k == 15):
                        exponentials(t + 2, 2 * k + 2)
                    high_tile(t + 1, 2 * k + 1)
                    if not (last and k == 15):
                        exponentials(t + 3, 2 * k + 3)
                if not (first and k == 0) and not (last and k == 17):
                    high_out(c - 1, (k - 1) % 2)
                if k == 14:
                    act.wait_ge(ln_stored, (i + 1) * 32)
                    act.wait_ge(mx_stored, (i + 1) * 16)

            steps(act, step)

            def gelu(g, f, first):
                act.wait_ge(up_ready, g * FT + f + 1)
                if not (first and f < 2):
                    act.wait_ge(g_lo_ready, g * FT + f - 1)
                nc.scalar.activation(g_full[:, f % 2, :], up_ps[f % 2], ACT.Gelu_apprx_tanh,
                                     bias=up_bias[:, f:f + 1]).then_inc(gelu_ready, 1)

            act.wait_ge(bias_loaded, 32)
            for f in range(FT):
                gelu(0, f, True)
            with act.Fori(1, GROUPS_FF) as g:
                for f in range(FT):
                    gelu(g, f, False)

        @block.vector
        def _(dve):
            def v_low(p, n, parity, bank):
                dve.wait_ge(v_hi_ready, p * 4 + n + 1)
                hi = v_hi[:, parity, 2 * n:2 * n + 2, :]
                nc.vector.tensor_tensor(v_lo[:, parity, 2 * n:2 * n + 2, :], bank.rearrange("p (a b) -> p a b", a=2),
                                        hi.bitcast(F32), ALU.subtract).then_inc(v_lo_ready, 1)

            def row_max(t, k2):
                dve.wait_ge(scores_ready, t + 1)
                nc.vector.tensor_reduce(neg_max[:, k2 % 16:k2 % 16 + 1], s_ps[k2 % 2][:, :], AXX, ALU.max,
                                        negate=True).then_inc(max_ready, 1)

            def low_tile(t, k2):
                for h in range(2):
                    dve.wait_ge(pt_hi_ready, t * 2 + h + 1)
                    at = (slice(None), (k2 // 2) % 2, slice(4 * h, 4 * h + 4), slice((k2 % 2) * P, (k2 % 2 + 1) * P))
                    nc.vector.tensor_tensor(pt_lo[at], t_ps[h][:, :, :], pt_hi[at].bitcast(F32),
                                            ALU.subtract).then_inc(pt_lo_ready, 1)

            def invert(c, k2):
                dve.wait_ge(probs_ready, c * 2 + 2)
                at = slice(k2 % 16, k2 % 16 + 2)
                nc.vector.reciprocal(inv_sum[:, at], row_sum[:, at]).then_inc(inv_ready, 1)

            def low_out(c, slot):
                dve.wait_ge(o_hi_ready, c + 1)
                nc.vector.tensor_tensor(o_lo[:, slot, :], o_ps[:, 0:CHUNK], o_hi[:, slot, :].bitcast(F32),
                                        ALU.subtract).then_inc(o_lo_ready, 1)

            def add_out(c, k, b):
                dve.wait_ge(out_ready, c + 1)
                dve.wait_ge(inv_ready, c + 1)
                dve.wait_ge(y_loaded[k % 4], (b + 1) * 16)
                for n in range(2):
                    col = (2 * k + n) % 16
                    rows = y[:, 2 * (k % 4) + n, :]
                    last = nc.vector.scalar_tensor_tensor(rows, w_ps[:, n * DIM:(n + 1) * DIM], inv_sum[:, col:col + 1],
                                                          rows, ALU.mult, ALU.add)
                last.then_inc(y_added, 1)

            LN_OWN = 5

            def mean(n, x, tiles):
                nc.vector.tensor_reduce(ln_mean[:, 0:tiles], x, AXX, ALU.add).then_inc(ln_link, 1)
                dve.wait_ge(ln_link, n * LN_OWN + 1)
                nc.vector.tensor_scalar(ln_mean[:, 0:tiles], ln_mean[:, 0:tiles], -1.0 / DIM, None,
                                        ALU.mult).then_inc(ln_mean_ready, 1)

            def variance(n, tiles, squares_before):
                dve.wait_ge(ln_sq_ready, squares_before + tiles)
                nc.vector.tensor_scalar(ln_var[:, 0:tiles], ln_sq[:, 0:tiles], 1.0 / DIM, EPS, ALU.mult,
                                        ALU.add).then_inc(ln_var_ready, 1)

            def normalise(n, x, out, tiles):
                at = slice(0, tiles)
                dve.wait_ge(ln_guess_ready, n + 1)
                nc.vector.tensor_tensor(ln_step[:, at], ln_guess[:, at], ln_guess[:, at], ALU.mult).then_inc(ln_link, 1)
                dve.wait_ge(ln_link, n * LN_OWN + 2)
                nc.vector.tensor_tensor(ln_step[:, at], ln_step[:, at], ln_var[:, at], ALU.mult).then_inc(ln_link, 1)
                dve.wait_ge(ln_link, n * LN_OWN + 3)
                nc.vector.tensor_scalar(ln_step[:, at], ln_step[:, at], -0.5, 1.5, ALU.mult, ALU.add).then_inc(ln_link, 1)
                dve.wait_ge(ln_link, n * LN_OWN + 4)
                nc.vector.tensor_tensor(ln_rstd[:, at], ln_guess[:, at], ln_step[:, at], ALU.mult).then_inc(ln_link, 1)
                dve.wait_ge(ln_link, n * LN_OWN + 5)
                for t in range(tiles):
                    last = nc.vector.tensor_scalar(out[:, t, :], x[:, t, :], ln_mean[:, t:t + 1], ln_rstd[:, t:t + 1],
                                                   ALU.add, ALU.mult)
                last.then_inc(ln_xn_ready, 1)

            blocks = lambda a: a[:, :].rearrange("p (a b) -> p a b", b=BLOCK)
            wide = lambda a: a[:, :].rearrange("p (a o) -> p a o", o=1).to_broadcast([P, MX_STEP // BLOCK, BLOCK])
            MX_OWN = 17

            def quantise(i, part):
                def link(n, ins):
                    ins.then_inc(mx_link, 1)
                    dve.wait_ge(mx_link, i * MX_OWN + n)

                at_least = lambda mid: nc.vector.scalar_tensor_tensor(
                    mx_q[:, :], mx_abs[:, :], mid, mx_q[:, :], ALU.is_ge, ALU.add)
                if part == 0:
                    dve.wait_ge(mx_loaded, (i + 1) * 16)
                    link(1, nc.vector.tensor_scalar(mx_abs[:, :].bitcast(U32), mx_raw[:, :].bitcast(U32), 0x7FFFFFFF,
                                                    None, ALU.bitwise_and))
                    link(2, nc.vector.tensor_reduce(mx_amax[:, :], blocks(mx_abs), AXX, ALU.max))
                if part == 1:
                    link(3, nc.vector.tensor_scalar(mx_amax[:, :], mx_amax[:, :], 1e-30, None, ALU.max))
                    link(4, nc.vector.tensor_scalar(mx_amax[:, :].bitcast(U32), mx_amax[:, :].bitcast(U32), 0x7F800000,
                                                    None, ALU.bitwise_and))
                    link(5, nc.vector.tensor_scalar(mx_half[:, :], mx_amax[:, :], 0.125, None, ALU.mult))
                    link(6, nc.vector.reciprocal(mx_inv[:, :], mx_amax[:, :]))
                    link(7, nc.vector.tensor_scalar(mx_inv[:, :], mx_inv[:, :], 4.0, None, ALU.mult))
                if part == 2:
                    link(8, nc.vector.tensor_tensor(blocks(mx_abs), blocks(mx_abs), wide(mx_inv), ALU.mult))
                    link(9, nc.vector.tensor_scalar(mx_q[:, :], mx_abs[:, :], 5.0, 2.0, ALU.is_ge, ALU.mult))
                if part == 3:
                    link(10, at_least(3.5))
                    link(11, at_least(2.5))
                if part == 4:
                    link(12, nc.vector.tensor_scalar(mx_q[:, :], mx_q[:, :], 2.0, None, ALU.mult))
                    link(13, at_least(1.75))
                if part == 5:
                    link(14, at_least(1.25))
                    link(15, at_least(0.75))
                if part == 6:
                    nc.vector.tensor_scalar(mx_raw[:, :].bitcast(U32), mx_raw[:, :].bitcast(U32), 0x80000000, None,
                                            ALU.bitwise_and)
                    link(16, at_least(0.25))
                if part == 7:
                    link(17, nc.vector.tensor_tensor(blocks(mx_q), blocks(mx_q), wide(mx_half), ALU.mult))
                    nc.vector.tensor_tensor(mx_q[:, :].bitcast(U32), mx_raw[:, :].bitcast(U32), mx_q[:, :].bitcast(U32),
                                            ALU.bitwise_or).then_inc(mx_ready, 1)

            for c in range(4):
                dve.wait_ge(y_loaded[c], 16)
            xn_first = probs[:, 0:2, :].rearrange("p a (b c) -> p (a b) c", c=DIM)
            mean(0, y[:, :, :], BT)
            variance(0, BT, 0)
            normalise(0, y, xn_first, BT)
            for n in range(4):
                dve.wait_ge(first_hi, n + 1)
                cols = slice((n % 2) * HALF, (n % 2 + 1) * HALF)
                nc.vector.tensor_tensor(x_lo[:, n // 2, cols], s_ps[n // 2][:, cols], x_hi[:, n // 2, cols].bitcast(F32),
                                        ALU.subtract).then_inc(x_ready, 8)
            dve.wait_ge(const_loaded, 32)
            for (place, part, n), bank in zip(FIRST_GROUPS, FIRST_BANKS):
                if part == "v":
                    v_low(0, n, 0, bank)
                if part == "qk0":
                    rotate(dve, nc.vector, 0, "qk0", n)
            row_max(0, 0)
            row_max(1, 1)

            def step(i, k, first, last):
                c = i * 16 + k
                t = c * 2
                tail = last and k >= 16
                has_out = not (first and k < 2)
                g = None if tail or (first and k == 0) else group_at(k - 1, 1, last)
                if g and g[1] == "v":
                    v_low(i * 2 + g[3], g[2], g[3] % 2, w_ps[:, :])
                if (k - 1, 1) == LN_SLOT:
                    dve.wait_ge(ln_hi_ready, i + 1)
                    nc.vector.tensor_tensor(ln_lo[:, :, :], w_ps[:, :].rearrange("p (a b) -> p a b", a=CT),
                                            ln_hi[:, :, :].bitcast(F32), ALU.subtract).then_inc(ln_lo_ready, 1)
                if not tail:
                    low_tile(t, 2 * k)
                    if not (last and k == 15):
                        row_max(t + 2, 2 * k + 2)
                if k == 1:
                    variance(i + 1, LN_STEP, i * LN_STEP + BT)
                if k == 2:
                    normalise(i + 1, ln_x, ln_xn, LN_STEP)
                if has_out:
                    invert(c - 2, 2 * k - 4)
                if not tail:
                    g = group_at(k, 0, last)
                    if g and g[1] == "v":
                        v_low(i * 2 + g[3], g[2], g[3] % 2, w_ps[:, :])
                    if not (last and k == 15):
                        row_max(t + 3, 2 * k + 3)
                if has_out:
                    add_out(c - 2, (k - 2) % 16, (i // 4) if k >= 2 else ((i - 1) // 4))
                if not tail:
                    low_tile(t + 1, 2 * k + 1)
                if not (first and k == 0) and not (last and k == 17):
                    low_out(c - 1, (k - 1) % 2)
                if k == 0:
                    dve.wait_ge(ln_loaded, (i + 1) * 16)
                    mean(i + 1, ln_x[:, :, :], LN_STEP)
                if k in MX_PARTS:
                    quantise(i, MX_PARTS.index(k))

            steps(dve, step)

            def split_gelu(g, f, first):
                dve.wait_ge(gelu_ready, g * FT + f + 1)
                if not (first and f < 4):
                    dve.wait_ge(down_ready, g * FT + f - 3)
                nc.vector.tensor_copy(g_hi[:, f % 4, :], g_full[:, f % 2, :]).then_inc(g_hi_ready, 1)
                dve.wait_ge(g_hi_ready, g * FT + f + 1)
                nc.vector.tensor_tensor(g_lo[:, f % 4, :], g_full[:, f % 2, :], g_hi[:, f % 4, :].bitcast(F32),
                                        ALU.subtract).then_inc(g_lo_ready, 1)

            def sum_rows(g, n, h, rounds):
                if h == 0:
                    dve.wait_ge(y_stored, 64 * BATCH)
                    dve.wait_ge(down_ready, g * FT + FT)
                    dve.wait_ge(y_biased, g + 1)
                    if not (isinstance(rounds, int) and rounds == 0):
                        dve.wait_ge(out_stored[n], rounds * 16)
                rows = slice(2 * h, 2 * h + 2)
                nc.vector.tensor_tensor(y_out[:, n, rows], y_ps[n][:, rows], y_in[:, n, rows], ALU.add).then_inc(rows_ready, 1)

            def group(b, n):
                g, first = b * 2 + n, isinstance(b, int) and b == 0 and n == 0
                for f in range(FT):
                    split_gelu(g, f, first)
                    if f in (1, 2) and not first:
                        sum_rows(g - 1, 1 - n, f - 1, b if n == 1 else b - 1)

            for b in range(2):
                group(b, 0)
                group(b, 1)
            with dve.Fori(2, BATCH) as b:
                group(b, 0)
                group(b, 1)
            for h in range(2):
                sum_rows(GROUPS_FF - 1, 1, h, BATCH - 1)

        @block.tensor
        def _(pe):
            def chain(out, terms, inc=None):
                for n, (w, m) in enumerate(terms):
                    ins = nc.tensor.matmul(out, w, m, start=(n == 0), stop=(n == len(terms) - 1))
                if inc is not None:
                    ins.then_inc(inc, 1)

            def project(part, n, bank):
                if part == "v":
                    cols = PARTS["v"]
                    for t in range(2):
                        tok = slice((2 * n + t) * P, (2 * n + t + 1) * P)
                        chain(bank[:, t * 256:(t + 1) * 256],
                              [term for c in range(CT) for term in
                               ((x_hi[:, c, tok], w_hi[:, c, cols]), (x_hi[:, c, tok], w_lo[:, c, cols]),
                                (x_lo[:, c, tok], w_hi[:, c, cols]))],
                              proj_ready if t == 1 else None)
                    return
                _, kind, half = qk_slot(part, n)
                col = PARTS[part].start + kind * HEAD
                cols, tok = slice(col, col + HEAD), slice(half * HALF, (half + 1) * HALF)
                chain(bank, [term for c in range(CT) for term in
                             ((w_hi[:, c, cols], x_hi[:, c, tok]), (w_hi[:, c, cols], x_lo[:, c, tok]),
                              (w_lo[:, c, cols], x_hi[:, c, tok]))], proj_ready)

            def bank_free(i, k, slot, first, last):
                before = [(k, s) for s in range(slot)][::-1] + [(k - n, s) for n in (1, 2) for s in (2, 1, 0)]
                for kk, s in before:
                    if s == 1:
                        if first and kk < 2:
                            continue
                        pe.wait_ge(y_added, i * 16 + kk - 1)
                        return
                    if (kk, s // 2) == LN_SLOT:
                        pe.wait_ge(ln_lo_ready, i + 1)
                        return
                    if (kk, s // 2) == MX_SLOT:
                        pe.wait_ge(mx_copied, i + 1)
                        return
                    g = group_at(kk % 16, s // 2, last and kk >= 0)
                    if g:
                        p = i * 2 + g[3] - (2 if kk < 0 else 0)
                        if g[1] == "v":
                            pe.wait_ge(v_lo_ready, p * 4 + g[2] + 1)
                        else:
                            pe.wait_ge(rope_in, p * 8 + qk_number(g[1], g[2]) + 1)
                        return

            def scores(k2, p, tile_ready):
                head = (k2 // 8) % 2
                if tile_ready:
                    pe.wait_ge(qk_ready, p * 8 + 4 * (head + 1))
                tile = (k2 % 8) * P
                q_hi, q_lo = qk_hi[:, head, 0, tile:tile + P], qk_lo[:, head, 0, tile:tile + P]
                for h in range(2):
                    keys = slice(h * HALF, (h + 1) * HALF)
                    k_hi, k_lo = qk_hi[:, head, 1, keys], qk_lo[:, head, 1, keys]
                    chain(s_ps[k2 % 2][:, keys], ((q_hi, k_hi), (q_hi, k_lo), (q_lo, k_hi)),
                          scores_ready if h == 1 else None)

            def turn(t, k2, first):
                pe.wait_ge(probs_ready, t + 1)
                for h in range(2):
                    if not first:
                        pe.wait_ge(pt_lo_ready, t * 2 + h - 1)
                    for j in range(4):
                        kt = 4 * h + j
                        ins = nc.tensor.transpose(t_ps[h][:, j, :], probs[:, k2 % 4, kt * P:(kt + 1) * P], ident[:, :])
                    ins.then_inc(pt_ready, 1)

            def values(c, k, p, first):
                pe.wait_ge(pt_lo_ready, c * 4 + 4)
                if not first:
                    pe.wait_ge(o_lo_ready, c)
                if k % 8 == 0:
                    pe.wait_ge(v_lo_ready, p * 4 + 4)
                parity, head, slot = (k // 8) % 2, (k // 4) % 2, k % 2
                cols = slice(head * HEAD, (head + 1) * HEAD)
                chain(o_ps[:, 0:CHUNK],
                      [term for kt in range(BT) for term in
                       ((v_hi[:, parity, kt, cols], pt_hi[:, slot, kt, :]), (v_hi[:, parity, kt, cols], pt_lo[:, slot, kt, :]),
                        (v_lo[:, parity, kt, cols], pt_hi[:, slot, kt, :]))], o_ready)

            def output(c, k, p):
                head, slot = (k // 4) % 2, k % 2
                pe.wait_ge(o_lo_ready, c + 1)
                if k % 4 == 0:
                    pe.wait_ge(wo_lo_ready[head], p + 1)
                for n in range(2):
                    rows = slice(n * P, (n + 1) * P)
                    chain(w_ps[:, n * DIM:(n + 1) * DIM],
                          ((o_hi[:, slot, rows], wo_hi[:, head, :]), (o_hi[:, slot, rows], wo_lo[:, head, :]),
                           (o_lo[:, slot, rows], wo_hi[:, head, :])), out_ready if n == 1 else None)

            down_blocks = down_w.rearrange("p (m f n) -> p m f n", m=CT, f=FT)
            seq_cols = seq_parts[:, :, :, :, :].rearrange("p b h c s -> p (b h c s)")

            def up(b, n, f):
                if isinstance(b, int) and b == 0 and n == 0 and f < 2:
                    if f == 0:
                        pe.wait_ge(mx_w_loaded[0], 16)
                        pe.wait_ge(x_ready, (BATCH + 1) * 32)
                else:
                    pe.wait_ge(gelu_ready, b * 2 * FT + n * FT + f - 1)
                for m in range(2 * CT):
                    c, part = m // 2, m % 2
                    block_at = (2 * f + c) * P
                    at = b * (2 * CT * SEQ) + ((part * CT + c) * SEQ + n * HALF)
                    ins = nc.tensor.matmul(up_ps[f % 2], up_w[:, block_at:block_at + P], seq_cols[:, bass.ds(at, HALF)],
                                           start=(m == 0), stop=(m == 2 * CT - 1))
                ins.then_inc(up_ready, 1)

            def down(b, n, f):
                pe.wait_ge(g_lo_ready, (b * 2 + n) * FT + f + 1)
                if f == 0 and not (isinstance(b, int) and b == 0):
                    pe.wait_ge(rows_ready, (b * 2 + n - 1) * 2)
                for t in range(GT):
                    for m, part in enumerate((g_hi, g_lo)):
                        ins = nc.tensor.matmul(y_ps[n][:, t, :], part[:, f % 4, t * P:(t + 1) * P], down_blocks[:, :, f, :],
                                               start=(f == 0 and m == 0 and t % 2 == 0),
                                           stop=(f == FT - 1 and m == 1 and t % 2 == 1))
                ins.then_inc(down_ready, 1)

            pe.wait_ge(ident_loaded, 16)
            pe.wait_ge(ln_xn_ready, 1)
            xn_first = probs[:, 0:2, :].rearrange("p a (b c) -> p (a b) c", c=DIM)
            for n in range(4):
                for j in range(4):
                    ins = nc.tensor.transpose(s_ps[n // 2][:, (n % 2) * HALF + j * P:(n % 2) * HALF + (j + 1) * P],
                                              xn_first[:, (n % 2) * 4 + j, (n // 2) * P:(n // 2 + 1) * P], ident[:, :])
                ins.then_inc(first_turned, 1)
            pe.wait_ge(x_ready, 32)
            for m, ((place, part, n), bank) in enumerate(zip(FIRST_GROUPS, FIRST_BANKS)):
                pe.wait_ge(w_lo_ready[part], 1)
                if m >= 6:
                    _, old_part, old_n = FIRST_GROUPS[m - 6 if m < 8 else m - 4]
                    if old_part == "v":
                        pe.wait_ge(v_lo_ready, old_n + 1)
                    else:
                        pe.wait_ge(rope_in, qk_number(old_part, old_n) + 1)
                project(part, n, bank)
            scores(0, 0, True)
            pe.wait_ge(v_lo_ready, 1)
            scores(1, 0, False)

            def step(i, k, first, last):
                c = i * 16 + k
                t = c * 2
                tail = last and k >= 16

                def next_scores(n):
                    if last and k == 15:
                        return
                    k2 = 2 * k + 2 + n
                    scores(k2, i * 2 + k2 // 16, k2 % 8 == 0)

                def slot(n):
                    if (k, n) == LN_SLOT:
                        bank_free(i, k, 2 * n, first, last)
                        pe.wait_ge(ln_xn_ready, i + 2)
                        for m in range(CT * LN_STEP):
                            ins = nc.tensor.transpose(w_ps[:, m * P:(m + 1) * P],
                                                      ln_xn[:, m % LN_STEP, (m // LN_STEP) * P:(m // LN_STEP + 1) * P], ident[:, :])
                        ins.then_inc(ln_turned, 1)
                        return
                    if (k, n) == MX_SLOT:
                        bank_free(i, k, 2 * n, first, last)
                        pe.wait_ge(mx_ready, i + 1)
                        for m in range(MX_STEP // P):
                            ins = nc.tensor.transpose(w_ps[:, m * P:(m + 1) * P], mx_q[:, m * P:(m + 1) * P], ident[:, :])
                        ins.then_inc(mx_turned_ready, 1)
                        return
                    g = group_at(k, n, last)
                    if not g:
                        return
                    place, part, num, ahead = g
                    if first and k == 0:
                        pe.wait_ge(rope_in, 6)
                        pe.wait_ge(v_lo_ready, 4)
                    else:
                        bank_free(i, k, 2 * n, first, last)
                    if num == 0:
                        pe.wait_ge(w_lo_ready[part], i * 2 + ahead + 1)
                    if place == 0 and ahead == 2:
                        pe.wait_ge(x_ready, ((i + 1) // 4 + 1) * 32)
                    project(part, num, w_ps[:, :])

                if tail:
                    up(0, 0, k - 16)
                if not tail:
                    turn(t, 2 * k, first and k == 0)
                    next_scores(0)
                    slot(0)
                    turn(t + 1, 2 * k + 1, False)
                    next_scores(1)
                if not (first and k < 2):
                    bank_free(i, k, 1, first, last)
                    output(c - 2, (k - 2) % 16, i * 2 + (k - 2) // 8)
                if not (first and k == 0) and not (last and k == 17):
                    values(c - 1, (k - 1) % 16, i * 2 + (k - 1) // 8, first and k == 1)
                if not tail:
                    slot(1)

            steps(pe, step)

            def group(b, n, final):
                for f in range(FT):
                    if f < FT - 2:
                        up(b, n, f + 2)
                    elif n == 0:
                        up(b, 1, f + 2 - FT)
                    elif not final:
                        up(b + 1, 0, f + 2 - FT)
                    down(b, n, f)

            pe.wait_ge(mx_w_loaded[1], 16)
            group(0, 0, False)
            pe.wait_ge(seq_loaded[1], 32)
            group(0, 1, False)
            with pe.Fori(1, BATCH - 1) as b:
                group(b, 0, False)
                for n in range(2, BATCH):
                    pe.wait_ge(seq_loaded[n], 32)
                group(b, 1, False)
            group(BATCH - 1, 0, False)
            group(BATCH - 1, 1, True)


def _rope_tables():
    inv = (np.float32(1.0) / np.power(np.float32(10000.0), np.arange(0, HEAD, 2, dtype=np.float32) / np.float32(HEAD))).astype(np.float32)
    angle = (np.arange(SEQ, dtype=np.float32)[None, :] * inv[:, None]).astype(np.float32)
    cos, sin = np.cos(angle.astype(np.float64)), np.sin(angle.astype(np.float64))
    return np.concatenate([cos, cos]).astype(np.float32), np.concatenate([-sin, sin]).astype(np.float32)


def build(nc, ins, outs):
    d = dict(ins)
    d["xnt"] = nc.dram_tensor("xnt_parts", [2, P, CT, TOK], F32, kind="Internal").ap()
    d["mx"] = nc.dram_tensor("mx_blocks", [P, MX_COLS], F32, kind="Internal").ap()
    d["y"] = nc.dram_tensor("x_plus_attention", [P, TILES, DIM], F32, kind="Internal").ap()
    d["out"] = outs["out"].rearrange("(t p) c -> p t c", p=P)
    d["x"] = ins["x"].rearrange("(t p) c -> p t c", p=P)
    layer(nc, d)


def kernel(L0_attn_x, L0_attn_w_qkv, L0_attn_w_out, L0_ffn_up_kernel, L0_ffn_up_bias, L0_ffn_down_kernel, L0_ffn_down_bias):
    import concourse.bacc as bacc
    from concourse.bass_utils import run_bass_kernel_spmd

    A = np.ascontiguousarray
    cos, sin = _rope_tables()
    w = np.asarray(L0_attn_w_qkv).reshape(3, HEADS // 2, 2, HEAD, CT, P)
    cols = [w[0, :, 0], w[1, :, 0], w[0, :, 1], w[1, :, 1], w[2, :, 0], w[2, :, 1]]
    w_qkv = np.concatenate(cols, axis=1).transpose(0, 3, 2, 1)
    w_out = np.asarray(L0_attn_w_out).reshape(DIM, HEADS // 2, 2, HEAD).transpose(1, 3, 2, 0)
    arrays = {
        "x": A(np.asarray(L0_attn_x).reshape(TOK, DIM)),
        "w_qkv": A(w_qkv),
        "w_out": A(w_out),
        "mx_rows": A(np.concatenate([
            np.asarray(L0_ffn_up_kernel).T.reshape(FT, P, DIM).transpose(1, 0, 2).reshape(P, FT * DIM),
            np.asarray(L0_ffn_down_kernel).T.reshape(CT, P, FF).transpose(1, 0, 2).reshape(P, CT * FF)], axis=1)),
        "up_bias": A(np.asarray(L0_ffn_up_bias).reshape(FT, P).T),
        "down_bias": A(np.asarray(L0_ffn_down_bias).reshape(1, DIM)),
        "cos": cos, "sin": sin, "ident": np.eye(P, dtype=np.float32),
    }
    nc = bacc.Bacc("TRN2", target_bir_lowering=False, num_devices=1)
    ins = {n: nc.dram_tensor(f"in_{n}", a.shape, mybir.dt.from_np(a.dtype), kind="ExternalInput").ap() for n, a in arrays.items()}
    outs = {"out": nc.dram_tensor("out_dram", (TOK, DIM), F32, kind="ExternalOutput").ap()}
    build(nc, ins, outs)
    r = run_bass_kernel_spmd(nc, [{f"in_{n}": a for n, a in arrays.items()}], core_ids=[0])
    return r.results[0]["out_dram"].reshape(BATCH, SEQ, DIM)
```

```python
import math
from contextlib import ExitStack

import numpy as np

import concourse.bass as bass
from concourse import mybir

F32 = mybir.dt.float32
F32R = mybir.dt.float32r
U32 = mybir.dt.uint32
ACT = mybir.ActivationFunctionType
ALU = mybir.AluOpType
AXX = mybir.AxisListType.X

BATCH, SEQ, DIM = 4, 1024, 256
HEADS, HEAD = 16, 128
FF = 1024
P = 128
TOK = BATCH * SEQ
TILES = TOK // P
BT = SEQ // P
CT = DIM // P
FT = FF // P
BLOCK = 32
SCALE = 1.0 / math.sqrt(HEAD)
EPS = 1e-5
HALF = SEQ // 2
PAIRS = BATCH * HEADS // 2
PAIRS_PER_SEQ = HEADS // 2
CHUNK = 2 * P
QUARTERS = SEQ // CHUNK
SEQ_CHUNKS = HEADS * QUARTERS
PAIR_GROUPS = 12
WCOLS = 6 * HEAD
MX_COLS = 2 * DIM * FF // P
ROUNDS = PAIRS // 2
SEQ_ROUNDS = PAIRS_PER_SEQ // 2
MX_STEP = MX_COLS // ROUNDS
LN_STEP = TILES // ROUNDS


def layer(nc, d):
    with ExitStack() as ctx:
        def sb(name, shape, dt=F32):
            return ctx.enter_context(nc.sbuf_tensor(name, shape, dt))

        def sem(name):
            return ctx.enter_context(nc.semaphore(name))

        def pb(name, shape):
            return ctx.enter_context(nc.psum_tensor(name, shape, F32))

        ident = sb("ident", [P, P])
        cos = sb("cos", [P, SEQ])
        sin = sb("sin", [P, SEQ])
        seq_parts = sb("seq_parts", [P, BATCH, 2, CT, SEQ], F32R)
        x_hi, x_lo = seq_parts[:, 0, 0], seq_parts[:, 0, 1]
        w_raw = sb("w_raw", [P, CT, WCOLS])
        w_parts = sb("w_parts", [P, 2, CT, WCOLS], F32R)
        w_hi, w_lo = w_parts[:, 0], w_parts[:, 1]
        wo_raw = sb("wo_raw", [P, 2, DIM])
        wo_hi = sb("wo_hi", [P, 2, DIM], F32R)
        wo_lo = sb("wo_lo", [P, 2, DIM], F32R)
        qk_hi, qk_lo = seq_parts[:, 1], seq_parts[:, 2]
        v_hi = seq_parts[:, 3].rearrange("p a c (t n) -> p a (c t) n", n=2 * HEAD)
        v_lo = sb("v_lo", [P, 2, BT, 2 * HEAD], F32R)
        rope_a = sb("rope_a", [P, 2, HALF])
        rope_b = sb("rope_b", [P, 2, HALF])
        probs = sb("probs", [P, 4, SEQ])
        pt_hi = sb("pt_hi", [P, 2, BT, CHUNK], F32R)
        pt_lo = sb("pt_lo", [P, 2, BT, CHUNK], F32R)
        o_hi = sb("o_hi", [P, 2, CHUNK], F32R)
        o_lo = sb("o_lo", [P, 2, CHUNK], F32R)
        y = sb("y", [P, BT, DIM])
        neg_max = sb("neg_max", [P, 16])
        row_sum = sb("row_sum", [P, 16])
        inv_sum = sb("inv_sum", [P, 16])
        ln_x = sb("ln_x", [P, LN_STEP, DIM])
        ln_xn = sb("ln_xn", [P, LN_STEP, DIM])
        ln_hi = sb("ln_hi", [P, CT, LN_STEP * P], F32R)
        ln_lo = sb("ln_lo", [P, CT, LN_STEP * P], F32R)
        ln_mean = sb("ln_mean", [P, BT])
        ln_sq = sb("ln_sq", [P, BT])
        ln_var = sb("ln_var", [P, BT])
        ln_guess = sb("ln_guess", [P, BT])
        ln_step = sb("ln_step", [P, BT])
        ln_rstd = sb("ln_rstd", [P, BT])
        minus_half = sb("minus_half", [P, BT])
        mx_raw = sb("mx_raw", [P, MX_STEP])
        mx_abs = sb("mx_abs", [P, MX_STEP])
        mx_q = sb("mx_q", [P, MX_STEP])
        mx_amax = sb("mx_amax", [P, MX_STEP // BLOCK])
        mx_half = sb("mx_half", [P, MX_STEP // BLOCK])
        mx_inv = sb("mx_inv", [P, MX_STEP // BLOCK])
        mx_turned = sb("mx_turned", [P, MX_STEP])

        up_w = sb("up_w", [P, MX_COLS // 2], F32R)
        down_w = w_parts[:, :, :, :].rearrange("p a b c -> p (a b c)")[:, 0:MX_COLS // 2]
        g_full = probs[:, 0, :].rearrange("p (a b) -> p a b", a=2)
        g_hi, g_lo = (t[:, 0].rearrange("p (f a) c -> p f (a c)", f=4) for t in (pt_hi, pt_lo))
        y_in = probs[:, 1:3, :].rearrange("p s (t c) -> p s t c", c=DIM)
        y_out = y[:, :, :].rearrange("p (s t) c -> p s t c", s=2)
        up_bias = sb("up_bias", [P, FT])
        down_bias = sb("down_bias", [P, DIM])

        s_ps = [pb(f"s_ps{i}", [P, SEQ]) for i in range(2)]
        turn_ps = pb("turn_ps", [P, 2, 4, P])
        t_ps = [turn_ps[:, 0], turn_ps[:, 1]]
        up_ps = [s_ps[0][:, 0:HALF], s_ps[0][:, HALF:SEQ]]
        y_ps = [s_ps[1][:, :].rearrange("p (t c) -> p t c", c=DIM),
                turn_ps[:, :, :, :].rearrange("p a b c -> p (a b c)").rearrange("p (t c) -> p t c", c=DIM)]
        o_ps = pb("o_ps", [P, 512])
        w_ps = pb("w_ps", [P, 512])
        flat = lambda a: a[:, :, :].rearrange("p a b -> p (a b)")
        FIRST_BANKS = [w_ps[:, :], o_ps[:, :], s_ps[1][:, 0:512], s_ps[1][:, 512:1024], flat(t_ps[0]), flat(t_ps[1]),
                       w_ps[:, :], o_ps[:, :], flat(t_ps[0]), s_ps[1][:, 0:512]]
        FIRST_HELD = {6: 0, 7: 1, 8: 4, 9: 2}

        const_loaded = sem("const_loaded")
        ident_loaded = sem("ident_loaded")
        x_ready = sem("x_ready")
        PARTS = {"qk0": slice(0, 256), "qk1": slice(256, 512), "v": slice(512, 768)}
        w_loaded = {k: sem(f"w_loaded_{k}") for k in PARTS}
        w_hi_ready = {k: sem(f"w_hi_{k}") for k in PARTS}
        w_lo_ready = {k: sem(f"w_lo_{k}") for k in PARTS}
        wo_loaded = [sem(f"wo_loaded{i}") for i in range(2)]
        wo_hi_ready = [sem(f"wo_hi{i}") for i in range(2)]
        wo_lo_ready = [sem(f"wo_lo{i}") for i in range(2)]
        proj_ready = sem("proj_ready")
        rope_in = sem("rope_in")
        rope_step = {"pool": sem("rope_step"), "dve": sem("rope_step_dve")}
        first_keys_pool = sem("first_keys_pool")
        first_qk_dve = sem("first_qk_dve")
        qk_ready = sem("qk_ready")
        v_hi_ready = sem("v_hi_ready")
        v_lo_ready = sem("v_lo_ready")
        scores_ready = sem("scores_ready")
        max_ready = sem("max_ready")
        probs_ready = sem("probs_ready")
        pt_ready = sem("pt_ready")
        pt_hi_ready = sem("pt_hi_ready")
        pt_lo_ready = sem("pt_lo_ready")
        o_ready = sem("o_ready")
        o_hi_ready = sem("o_hi_ready")
        o_lo_ready = sem("o_lo_ready")
        inv_ready = sem("inv_ready")
        out_ready = sem("out_ready")
        y_added = sem("y_added")
        y_loaded = [sem(f"y_loaded{c}") for c in range(QUARTERS)]
        y_stored = sem("y_stored")
        ln_loaded = sem("ln_loaded")
        ln_sum_ready = sem("ln_sum_ready")
        ln_mean_ready = sem("ln_mean_ready")
        ln_sq_ready = sem("ln_sq_ready")
        ln_var_ready = sem("ln_var_ready")
        ln_guess_ready = sem("ln_guess_ready")
        ln_xn_ready = sem("ln_xn_ready")
        ln_turned = sem("ln_turned")
        ln_hi_ready = sem("ln_hi_ready")
        ln_lo_ready = sem("ln_lo_ready")
        ln_stored = sem("ln_stored")
        half_ready = sem("half_ready")
        first_turned = sem("first_turned")
        first_hi = sem("first_hi")
        ln_link = sem("ln_link")
        mx_loaded = sem("mx_loaded")
        mx_link = sem("mx_link")
        mx_ready = sem("mx_ready")
        mx_turned_ready = sem("mx_turned_ready")
        mx_copied = sem("mx_copied")
        mx_stored = sem("mx_stored")
        mx_w_loaded = [sem("up_w_loaded"), sem("down_w_loaded")]
        bias_loaded = sem("bias_loaded")
        seq_loaded = [None] + [sem(f"seq_loaded{b}") for b in range(1, BATCH)]
        y_in_loaded = [sem(f"y_in_loaded{n}") for n in range(2)]
        y_biased = sem("y_biased")
        up_ready = sem("up_ready")
        gelu_ready = sem("gelu_ready")
        g_hi_ready = sem("g_hi_ready")
        g_lo_ready = sem("g_lo_ready")
        down_ready = sem("down_ready")
        rows_ready = sem("rows_ready")
        out_stored = [sem(f"out_stored{n}") for n in range(2)]

        block = ctx.enter_context(nc.Block())

        GROUPS = {(3, 0): (0, "qk0", 0), (3, 1): (1, "qk0", 1), (4, 0): (2, "qk0", 2), (4, 1): (3, "v", 0),
                  (5, 0): (4, "qk0", 3), (5, 1): (5, "v", 1), (6, 0): (6, "v", 2), (6, 1): (7, "v", 3),
                  (7, 0): (8, "qk1", 0), (7, 1): (9, "qk1", 1), (0, 0): (10, "qk1", 2), (1, 0): (11, "qk1", 3)}
        FIRST_GROUPS = sorted(GROUPS.values())[:10]
        LN_SLOT, MX_SLOT = (2, 1), (10, 1)
        MX_PARTS = (2, 3, 4, 5, 6, 7, 8, 9)

        def group_at(k, slot, last):
            g = GROUPS.get((k % 8, slot))
            if g is None:
                return None
            ahead = k // 8 + (1 if k % 8 >= 3 else 0)
            if last and ahead > 1:
                return None
            return (*g, ahead)

        def qk_number(part, n):
            return n + (4 if part == "qk1" else 0)

        def qk_slot(part, n):
            return (0 if part == "qk0" else 1), 1 - n // 2, n % 2

        PEELED = 4

        def steps(eng, step):
            for k in range(PEELED):
                step(0, k, True, False)
            with eng.Fori(0, ROUNDS - 1) as i:
                for k in range(PEELED, PEELED + 16):
                    if k < 16:
                        step(i, k, False, False)
                    else:
                        step(i + 1, k - 16, False, False)
            for k in range(PEELED, 18):
                step(ROUNDS - 1, k, False, True)

        GROUPS_FF = TOK // HALF
        GT = HALF // P

        FIRST_HALVES = (slice(0, BT // 2), slice(BT // 2, BT))
        LN_COLS = slice(0, LN_STEP)

        def ln_tile(i):
            return (i * LN_STEP + BT) % TILES

        @block.sync
        def _(sp):
            def load_part(p, pw, part, first=False):
                if not first:
                    sp.wait_ge(w_lo_ready[part], p)
                    sp.wait_ge(w_hi_ready[part], p)
                sp.dma_start(w_raw[:, :, PARTS[part]], d["w_qkv"][pw][:, :, PARTS[part]]).then_inc(w_loaded[part], 16)

            def load_wo(p, pw, h, first=False):
                if not first:
                    sp.wait_ge(wo_lo_ready[h], p)
                    sp.wait_ge(wo_hi_ready[h], p)
                sp.dma_start(wo_raw[:, h, :], d["w_out"][pw][:, h, :]).then_inc(wo_loaded[h], 16)

            def load_x(b):
                cols = bass.ds(b * SEQ, SEQ)
                sp.dma_start(x_hi[:, :, :].bitcast(F32), d["xnt"][0][:, :, cols]).then_inc(x_ready, 16)
                sp.dma_start(x_lo[:, :, :].bitcast(F32), d["xnt"][1][:, :, cols]).then_inc(x_ready, 16)

            def load_y(b, c):
                sp.dma_start(y[:, 2 * c:2 * c + 2, :], d["x"][:, bass.ds(b * BT + 2 * c, 2), :]).then_inc(y_loaded[c], 16)

            def store_y(b, c):
                sp.wait_ge(y_added, b * SEQ_CHUNKS + (SEQ_CHUNKS - QUARTERS + 1 + c))
                sp.dma_start(d["y"][:, bass.ds(b * BT + 2 * c, 2), :], y[:, 2 * c:2 * c + 2, :]).then_inc(y_stored, 16)

            def load_ln(i):
                sp.dma_start(ln_x[:, :, :], d["x"][:, bass.ds(ln_tile(i), LN_STEP), :]).then_inc(ln_loaded, 16)

            def load_mx(i):
                sp.dma_start(mx_raw[:, :], d["mx_rows"][:, bass.ds(i * MX_STEP, MX_STEP)]).then_inc(mx_loaded, 16)

            def store_ln(i):
                sp.wait_ge(ln_lo_ready, i + 1)
                tok = bass.ds(ln_tile(i) * P, LN_STEP * P)
                sp.dma_start(d["xnt"][0][:, :, tok], ln_hi[:, :, :].bitcast(F32)).then_inc(ln_stored, 16)
                sp.dma_start(d["xnt"][1][:, :, tok], ln_lo[:, :, :].bitcast(F32)).then_inc(ln_stored, 16)

            def store_mx(i):
                sp.wait_ge(mx_copied, i + 1)
                sp.dma_start(d["mx"][:, bass.ds(i * MX_STEP, MX_STEP)], mx_turned[:, :]).then_inc(mx_stored, 16)

            for c in range(QUARTERS):
                load_y(0, c)
            load_part(0, 0, "qk0", True)
            sp.dma_start(ident[:, :], d["ident"]).then_inc(ident_loaded, 16)
            load_part(0, 0, "v", True)
            for name, dst in (("cos", cos), ("sin", sin)):
                sp.dma_start(dst[:, :], d[name]).then_inc(const_loaded, 16)
            load_part(0, 0, "qk1", True)
            load_wo(0, 0, 0, True)
            load_wo(0, 0, 1, True)
            load_ln(0)
            load_mx(0)

            def pair(b, j):
                p = b * PAIRS_PER_SEQ + j
                load_part(p, j, "qk0")
                load_part(p, j, "v")
                load_part(p, j, "qk1")
                rounds = b * SEQ_ROUNDS + j // 2
                if j % 2 == 0:
                    store_ln(rounds - 1)
                    load_ln(rounds)
                elif not isinstance(b, int) or j > 1:
                    store_mx(rounds - 1)
                    load_mx(rounds)
                if j == 0:
                    sp.wait_ge(ln_stored, b * (SEQ_ROUNDS * 32))
                load_wo(p, j, 0)
                if j == 0:
                    sp.wait_ge(proj_ready, b * (PAIRS_PER_SEQ * PAIR_GROUPS))
                    load_x(b)
                if j == 1 and not isinstance(b, int):
                    for c in range(QUARTERS):
                        store_y(b - 1, c)
                        sp.wait_ge(y_stored, (b - 1) * (QUARTERS * 16) + 16 * (c + 1))
                        load_y(b, c)
                load_wo(p, j, 1)

            for j in range(1, PAIRS_PER_SEQ):
                pair(0, j)
            with sp.Fori(1, BATCH) as b:
                for j in range(PAIRS_PER_SEQ):
                    pair(b, j)
            store_ln(ROUNDS - 1)
            store_mx(ROUNDS - 1)

            def load_seq(b):
                for part in range(2):
                    sp.dma_start(seq_parts[:, b, part].bitcast(F32),
                                 d["xnt"][part][:, :, b * SEQ:(b + 1) * SEQ]).then_inc(seq_loaded[b], 16)

            def load_rows(g, n):
                sp.dma_start(y_in[:, n], d["y"][:, bass.ds(g * GT, GT), :]).then_inc(y_in_loaded[n], 16)

            def store_rows(g, n):
                sp.wait_ge(rows_ready, (g + 1) * 2)
                sp.dma_start(d["out"][:, bass.ds(g * GT, GT), :], y_out[:, n]).then_inc(out_stored[n], 16)

            sp.dma_start(up_bias[:, :], d["up_bias"]).then_inc(bias_loaded, 16)
            sp.dma_start(down_bias[:, :], d["down_bias"].to_broadcast([P, DIM])).then_inc(bias_loaded, 16)
            sp.wait_ge(proj_ready, PAIRS * PAIR_GROUPS)
            sp.wait_ge(ln_stored, ROUNDS * 32)
            load_x(0)
            sp.wait_ge(mx_stored, ROUNDS * 16)
            for n in range(2):
                cols = slice(n * MX_COLS // 2, (n + 1) * MX_COLS // 2)
                dst = (up_w[:, :], down_w)[n]
                sp.dma_start(dst.bitcast(F32), d["mx"][:, cols]).then_inc(mx_w_loaded[n], 16)
            sp.wait_ge(scores_ready, TOK * HEADS // P)
            sp.wait_ge(pt_ready, TOK * HEADS // P * 2 - 2)
            for n in range(2):
                load_rows(n, n)
            load_seq(1)
            load_seq(2)
            sp.wait_ge(o_ready, PAIRS * 8)
            load_seq(3)
            for c in range(QUARTERS):
                store_y(BATCH - 1, c)
            sp.wait_ge(y_stored, BATCH * QUARTERS * 16)
            with sp.Fori(0, GROUPS_FF // 2 - 1) as b:
                for n in range(2):
                    store_rows(b * 2 + n, n)
                    load_rows(b * 2 + n + 2, n)
            for n in range(2):
                store_rows(GROUPS_FF - 2 + n, n)
            for n in range(2):
                sp.wait_ge(out_stored[n], 16 * (GROUPS_FF // 2))

        def rope_slot(p, m):
            if isinstance(p, int) and p == 0 and m == 3:
                return probs[:, 2, 0:HALF], probs[:, 2, HALF:SEQ]
            return rope_a[:, m % 2, :], rope_b[:, m % 2, :]

        def rotate(eng, engine, p, part, n, name, before):
            m = qk_number(part, n)
            head, kind, half = qk_slot(part, n)
            cols = slice(half * HALF, (half + 1) * HALF)
            a, b = rope_slot(p, m)
            hi, lo = qk_hi[:, head, kind, cols], qk_lo[:, head, kind, cols]
            own = rope_step[name]
            eng.wait_ge(rope_in, p * 8 + m + 1)
            engine.tensor_tensor(a, a, cos[:, cols], ALU.mult).then_inc(own, 1)
            engine.tensor_tensor(b, b, sin[:, cols], ALU.mult).then_inc(own, 1)
            eng.wait_ge(own, before * 4 + 2)
            engine.tensor_tensor(hi, a, b, ALU.add).then_inc(own, 1)
            eng.wait_ge(own, before * 4 + 3)
            engine.tensor_tensor(a, a, b, ALU.add).then_inc(own, 1)
            eng.wait_ge(own, before * 4 + 4)
            return engine.tensor_tensor(lo, a, hi.bitcast(F32), ALU.subtract)

        @block.gpsimd
        def _(pool):
            def w_low(p, part):
                cols = PARTS[part]
                pool.wait_ge(w_hi_ready[part], p + 1)
                nc.gpsimd.tensor_tensor(w_lo[:, :, cols], w_raw[:, :, cols], w_hi[:, :, cols].bitcast(F32),
                                        ALU.subtract).then_inc(w_lo_ready[part], 1)

            def wo_low(p, h):
                pool.wait_ge(wo_hi_ready[h], p + 1)
                nc.gpsimd.tensor_tensor(wo_lo[:, h, :], wo_raw[:, h, :], wo_hi[:, h, :].bitcast(F32),
                                        ALU.subtract).then_inc(wo_lo_ready[h], 1)

            def guess(n, at):
                pool.wait_ge(ln_var_ready, n + 1)
                nc.gpsimd.tensor_tensor(ln_guess[:, at], ln_var[:, at], minus_half[:, at], ALU.pow).then_inc(ln_guess_ready, 1)

            nc.gpsimd.memset(minus_half[:, :], -0.5).then_inc(half_ready, 1)
            pool.wait_ge(half_ready, 1)
            guess(0, FIRST_HALVES[0])
            guess(1, FIRST_HALVES[1])
            w_low(0, "qk0")
            w_low(0, "v")
            w_low(0, "qk1")
            wo_low(0, 0)
            pool.wait_ge(const_loaded, 32)
            rotate(pool, nc.gpsimd, 0, "qk0", 1, "pool", 0).then_inc(first_keys_pool, 1)
            for n in range(2):
                rotate(pool, nc.gpsimd, 0, "qk1", n, "pool", n + 1).then_inc(qk_ready, 1)

            def step(i, k, first, last):
                if k >= 16:
                    return
                k8 = k % 8
                more = not (last and k >= 8)
                p = i * 2 + k // 8
                if k8 == 0 and more:
                    w_low(p + 1, "qk0")
                    w_low(p + 1, "v")
                if k8 == 3:
                    wo_low(p, 1)
                if k8 == 4 and more:
                    w_low(p + 1, "qk1")
                if k8 == 6 and more:
                    wo_low(p + 1, 0)
                if k == 1:
                    guess(i + 2, LN_COLS)
                for slot in (0, 1):
                    g = group_at(k, slot, last)
                    if g and g[1] != "v":
                        p = i * 2 + g[3]
                        rotate(pool, nc.gpsimd, p, g[1], g[2], "pool", p * 8 + qk_number(g[1], g[2]) - 3).then_inc(qk_ready, 1)

            steps(pool, step)

            pool.wait_ge(bias_loaded, 32)
            with pool.Fori(0, GROUPS_FF // 2) as b:
                for n in range(2):
                    pool.wait_ge(y_in_loaded[n], (b + 1) * 16)
                    for t in range(GT):
                        ins = nc.gpsimd.tensor_tensor(y_in[:, n, t], y_in[:, n, t], down_bias[:, :], ALU.add)
                    ins.then_inc(y_biased, 1)

        @block.scalar
        def _(act):
            def w_high(p, part, first=False):
                cols = PARTS[part]
                act.wait_ge(w_loaded[part], (p + 1) * 16)
                if not first:
                    act.wait_ge(proj_ready, p * 12 - (0 if part == "qk1" else 4))
                nc.scalar.activation(w_hi[:, :, cols], w_raw[:, :, cols], ACT.Copy).then_inc(w_hi_ready[part], 1)

            def wo_high(p, h, first=False):
                act.wait_ge(wo_loaded[h], (p + 1) * 16)
                if not first:
                    act.wait_ge(out_ready, p * 8 - (4 if h == 0 else 0))
                nc.scalar.activation(wo_hi[:, h, :], wo_raw[:, h, :], ACT.Copy).then_inc(wo_hi_ready[h], 1)

            def take_group(p, place, part, n, parity, bank, first=False):
                act.wait_ge(proj_ready, p * 12 + place + 1)
                if part == "v":
                    nc.scalar.activation(v_hi[:, parity, 2 * n:2 * n + 2, :], bank.rearrange("p (a b) -> p a b", a=2),
                                         ACT.Copy).then_inc(v_hi_ready, 1)
                    return
                m = qk_number(part, n)
                if first and m in (2, 4):
                    act.wait_ge(first_qk_dve, m // 2)
                elif first and m == 5:
                    act.wait_ge(first_keys_pool, 1)
                elif not (first and m < 4):
                    act.wait_ge(qk_ready, p * 8 + m - 1)
                scale = SCALE if n // 2 == 1 else 1.0
                a, b = rope_slot(p, m)
                h = HEAD // 2
                nc.scalar.activation(a, bank, ACT.Copy, scale=scale)
                nc.scalar.activation(b[0:h], bank[h:P], ACT.Copy, scale=scale)
                nc.scalar.activation(b[h:P], bank[0:h], ACT.Copy, scale=scale).then_inc(rope_in, 1)

            def exponentials(t, k2):
                act.wait_ge(max_ready, t + 1)
                col = k2 % 16
                nc.scalar.activation(probs[:, k2 % 4, :], s_ps[k2 % 2][:, :], ACT.Exp, bias=neg_max[:, col:col + 1],
                                     accum_out=row_sum[:, col:col + 1]).then_inc(probs_ready, 1)

            def high_tile(t, k2):
                for h in range(2):
                    act.wait_ge(pt_ready, t * 2 + h + 1)
                    nc.scalar.activation(pt_hi[:, (k2 // 2) % 2, 4 * h:4 * h + 4, (k2 % 2) * P:(k2 % 2 + 1) * P],
                                         t_ps[h][:, :, :], ACT.Copy).then_inc(pt_hi_ready, 1)

            def high_out(c, slot):
                act.wait_ge(o_ready, c + 1)
                nc.scalar.activation(o_hi[:, slot, :], o_ps[:, 0:CHUNK], ACT.Copy).then_inc(o_hi_ready, 1)

            def squares(n, x, at):
                act.wait_ge(ln_mean_ready, n + 1)
                for t in range(at.start, at.stop):
                    if t >= LN_STEP:
                        act.wait_ge(ln_sq_ready, t - LN_STEP + 1)
                    nc.scalar.activation(ln_xn[:, t % LN_STEP, :], x[:, t, :], ACT.Square, bias=ln_mean[:, t:t + 1],
                                         accum_out=ln_sq[:, t:t + 1]).then_inc(ln_sq_ready, 1)

            squares(0, y, FIRST_HALVES[0])
            squares(1, y, FIRST_HALVES[1])
            w_high(0, "qk0", True)
            w_high(0, "v", True)
            for n in range(4):
                act.wait_ge(first_turned, n + 1)
                c, cols = n % 2, slice((n // 2) * HALF, (n // 2 + 1) * HALF)
                nc.scalar.activation(x_hi[:, c, cols], s_ps[c][:, cols], ACT.Copy).then_inc(first_hi, 1)
            w_high(0, "qk1", True)
            wo_high(0, 0, True)
            for (place, part, n), bank in zip(FIRST_GROUPS, FIRST_BANKS):
                take_group(0, place, part, n, 0, bank, True)
            exponentials(0, 0)
            exponentials(1, 1)

            def step(i, k, first, last):
                c = i * 16 + k
                t = c * 2
                p = i * 2 + k // 8
                more = not (last and k >= 8)
                tail = last and k >= 16
                if k % 8 == 0 and more and not tail:
                    w_high(p + 1, "qk0")
                    w_high(p + 1, "v")
                if k % 8 == 3:
                    wo_high(p, 1, first)
                if k % 8 == 4 and more:
                    w_high(p + 1, "qk1")
                if k % 8 == 6 and more:
                    wo_high(p + 1, 0)
                g = None if tail or (first and k == 0) else group_at(k - 1, 1, last)
                if g:
                    take_group(i * 2 + g[3], *g[:3], g[3] % 2, w_ps[:, :])
                if (k - 1, 1) == LN_SLOT:
                    act.wait_ge(ln_turned, i + 1)
                    nc.scalar.activation(ln_hi[:, :, :], w_ps[:, :].rearrange("p (a b) -> p a b", a=CT),
                                         ACT.Copy).then_inc(ln_hi_ready, 1)
                if (k - 1, 1) == MX_SLOT:
                    act.wait_ge(mx_turned_ready, i + 1)
                    nc.scalar.activation(mx_turned[:, :], w_ps[:, 0:MX_STEP], ACT.Copy).then_inc(mx_copied, 1)
                if not tail:
                    high_tile(t, 2 * k)
                    if k == 1:
                        squares(i + 2, ln_x, LN_COLS)
                    g = group_at(k, 0, last)
                    if g:
                        take_group(i * 2 + g[3], *g[:3], g[3] % 2, w_ps[:, :])
                    if not (last and k == 15):
                        exponentials(t + 2, 2 * k + 2)
                    high_tile(t + 1, 2 * k + 1)
                    if not (last and k == 15):
                        exponentials(t + 3, 2 * k + 3)
                if not (first and k == 0) and not (last and k == 17):
                    high_out(c - 1, (k - 1) % 2)
                if k == 14:
                    act.wait_ge(ln_stored, (i + 1) * 32)
                    act.wait_ge(mx_stored, (i + 1) * 16)

            steps(act, step)

            def gelu(g, f, first):
                act.wait_ge(up_ready, g * FT + f + 1)
                if not (first and f < 2):
                    act.wait_ge(g_lo_ready, g * FT + f - 1)
                nc.scalar.activation(g_full[:, f % 2, :], up_ps[f % 2], ACT.Gelu_apprx_tanh,
                                     bias=up_bias[:, f:f + 1]).then_inc(gelu_ready, 1)

            act.wait_ge(bias_loaded, 32)
            for f in range(FT):
                gelu(0, f, True)
            with act.Fori(1, GROUPS_FF) as g:
                for f in range(FT):
                    gelu(g, f, False)

        @block.vector
        def _(dve):
            def v_low(p, n, parity, bank):
                dve.wait_ge(v_hi_ready, p * 4 + n + 1)
                hi = v_hi[:, parity, 2 * n:2 * n + 2, :]
                nc.vector.tensor_tensor(v_lo[:, parity, 2 * n:2 * n + 2, :], bank.rearrange("p (a b) -> p a b", a=2),
                                        hi.bitcast(F32), ALU.subtract).then_inc(v_lo_ready, 1)

            def row_max(t, k2):
                dve.wait_ge(scores_ready, t + 1)
                nc.vector.tensor_reduce(neg_max[:, k2 % 16:k2 % 16 + 1], s_ps[k2 % 2][:, :], AXX, ALU.max,
                                        negate=True).then_inc(max_ready, 1)

            def low_tile(t, k2):
                for h in range(2):
                    dve.wait_ge(pt_hi_ready, t * 2 + h + 1)
                    at = (slice(None), (k2 // 2) % 2, slice(4 * h, 4 * h + 4), slice((k2 % 2) * P, (k2 % 2 + 1) * P))
                    nc.vector.tensor_tensor(pt_lo[at], t_ps[h][:, :, :], pt_hi[at].bitcast(F32),
                                            ALU.subtract).then_inc(pt_lo_ready, 1)

            def invert(c, k2):
                dve.wait_ge(probs_ready, c * 2 + 2)
                at = slice(k2 % 16, k2 % 16 + 2)
                nc.vector.reciprocal(inv_sum[:, at], row_sum[:, at]).then_inc(inv_ready, 1)

            def low_out(c, slot):
                dve.wait_ge(o_hi_ready, c + 1)
                nc.vector.tensor_tensor(o_lo[:, slot, :], o_ps[:, 0:CHUNK], o_hi[:, slot, :].bitcast(F32),
                                        ALU.subtract).then_inc(o_lo_ready, 1)

            def add_out(c, k, b):
                dve.wait_ge(out_ready, c + 1)
                dve.wait_ge(inv_ready, c + 1)
                dve.wait_ge(y_loaded[k % 4], (b + 1) * 16)
                for n in range(2):
                    col = (2 * k + n) % 16
                    rows = y[:, 2 * (k % 4) + n, :]
                    last = nc.vector.scalar_tensor_tensor(rows, w_ps[:, n * DIM:(n + 1) * DIM], inv_sum[:, col:col + 1],
                                                          rows, ALU.mult, ALU.add)
                last.then_inc(y_added, 1)

            LN_OWN = 4

            def mean(n, x, at):
                nc.vector.tensor_reduce(ln_mean[:, at], x[:, at, :], AXX, ALU.add).then_inc(ln_sum_ready, 1)
                dve.wait_ge(ln_sum_ready, n + 1)
                nc.vector.tensor_scalar(ln_mean[:, at], ln_mean[:, at], -1.0 / DIM, None, ALU.mult).then_inc(ln_mean_ready, 1)

            def variance(at, squares_before):
                dve.wait_ge(ln_sq_ready, squares_before + at.stop - at.start)
                nc.vector.tensor_scalar(ln_var[:, at], ln_sq[:, at], 1.0 / DIM, EPS, ALU.mult,
                                        ALU.add).then_inc(ln_var_ready, 1)

            def newton(n, at):
                dve.wait_ge(ln_guess_ready, n + 1)
                nc.vector.tensor_tensor(ln_step[:, at], ln_guess[:, at], ln_guess[:, at], ALU.mult).then_inc(ln_link, 1)
                dve.wait_ge(ln_link, n * LN_OWN + 1)
                nc.vector.tensor_tensor(ln_step[:, at], ln_step[:, at], ln_var[:, at], ALU.mult).then_inc(ln_link, 1)
                dve.wait_ge(ln_link, n * LN_OWN + 2)
                nc.vector.tensor_scalar(ln_step[:, at], ln_step[:, at], -0.5, 1.5, ALU.mult, ALU.add).then_inc(ln_link, 1)
                dve.wait_ge(ln_link, n * LN_OWN + 3)
                nc.vector.tensor_tensor(ln_rstd[:, at], ln_guess[:, at], ln_step[:, at], ALU.mult).then_inc(ln_link, 1)

            def normalise(n, x, out, at):
                dve.wait_ge(ln_link, n * LN_OWN + 4)
                for t in range(at.start, at.stop):
                    last = nc.vector.tensor_scalar(out[:, t, :], x[:, t, :], ln_mean[:, t:t + 1], ln_rstd[:, t:t + 1],
                                                   ALU.add, ALU.mult)
                last.then_inc(ln_xn_ready, 1)

            blocks = lambda a: a[:, :].rearrange("p (a b) -> p a b", b=BLOCK)
            wide = lambda a: a[:, :].rearrange("p (a o) -> p a o", o=1).to_broadcast([P, MX_STEP // BLOCK, BLOCK])
            MX_OWN = 17

            def quantise(i, part):
                def link(n, ins):
                    ins.then_inc(mx_link, 1)
                    dve.wait_ge(mx_link, i * MX_OWN + n)

                at_least = lambda mid: nc.vector.scalar_tensor_tensor(
                    mx_q[:, :], mx_abs[:, :], mid, mx_q[:, :], ALU.is_ge, ALU.add)
                if part == 0:
                    dve.wait_ge(mx_loaded, (i + 1) * 16)
                    link(1, nc.vector.tensor_scalar(mx_abs[:, :].bitcast(U32), mx_raw[:, :].bitcast(U32), 0x7FFFFFFF,
                                                    None, ALU.bitwise_and))
                    link(2, nc.vector.tensor_reduce(mx_amax[:, :], blocks(mx_abs), AXX, ALU.max))
                if part == 1:
                    link(3, nc.vector.tensor_scalar(mx_amax[:, :], mx_amax[:, :], 1e-30, None, ALU.max))
                    link(4, nc.vector.tensor_scalar(mx_amax[:, :].bitcast(U32), mx_amax[:, :].bitcast(U32), 0x7F800000,
                                                    None, ALU.bitwise_and))
                    link(5, nc.vector.tensor_scalar(mx_half[:, :], mx_amax[:, :], 0.125, None, ALU.mult))
                    link(6, nc.vector.reciprocal(mx_inv[:, :], mx_amax[:, :]))
                    link(7, nc.vector.tensor_scalar(mx_inv[:, :], mx_inv[:, :], 4.0, None, ALU.mult))
                if part == 2:
                    link(8, nc.vector.tensor_tensor(blocks(mx_abs), blocks(mx_abs), wide(mx_inv), ALU.mult))
                    link(9, nc.vector.tensor_scalar(mx_q[:, :], mx_abs[:, :], 5.0, 2.0, ALU.is_ge, ALU.mult))
                if part == 3:
                    link(10, at_least(3.5))
                    link(11, at_least(2.5))
                if part == 4:
                    link(12, nc.vector.tensor_scalar(mx_q[:, :], mx_q[:, :], 2.0, None, ALU.mult))
                    link(13, at_least(1.75))
                if part == 5:
                    link(14, at_least(1.25))
                    link(15, at_least(0.75))
                if part == 6:
                    nc.vector.tensor_scalar(mx_raw[:, :].bitcast(U32), mx_raw[:, :].bitcast(U32), 0x80000000, None,
                                            ALU.bitwise_and)
                    link(16, at_least(0.25))
                if part == 7:
                    link(17, nc.vector.tensor_tensor(blocks(mx_q), blocks(mx_q), wide(mx_half), ALU.mult))
                    nc.vector.tensor_tensor(mx_q[:, :].bitcast(U32), mx_raw[:, :].bitcast(U32), mx_q[:, :].bitcast(U32),
                                            ALU.bitwise_or).then_inc(mx_ready, 1)

            xn_first = probs[:, 0:2, :].rearrange("p a (b c) -> p (a b) c", c=DIM)
            for h, at in enumerate(FIRST_HALVES):
                dve.wait_ge(y_loaded[2 * h], 16)
                dve.wait_ge(y_loaded[2 * h + 1], 16)
                mean(h, y, at)
            variance(FIRST_HALVES[0], 0)
            newton(0, FIRST_HALVES[0])
            variance(FIRST_HALVES[1], BT // 2)
            normalise(0, y, xn_first, FIRST_HALVES[0])
            newton(1, FIRST_HALVES[1])
            normalise(1, y, xn_first, FIRST_HALVES[1])
            for n in range(4):
                dve.wait_ge(first_hi, n + 1)
                c, cols = n % 2, slice((n // 2) * HALF, (n // 2 + 1) * HALF)
                nc.vector.tensor_tensor(x_lo[:, c, cols], s_ps[c][:, cols], x_hi[:, c, cols].bitcast(F32),
                                        ALU.subtract).then_inc(x_ready, 8)
            dve.wait_ge(const_loaded, 32)
            rotate(dve, nc.vector, 0, "qk0", 0, "dve", 0).then_inc(first_qk_dve, 1)
            rotate(dve, nc.vector, 0, "qk0", 2, "dve", 1).then_inc(first_qk_dve, 1)
            for (place, part, n), bank in zip(FIRST_GROUPS, FIRST_BANKS):
                if part == "v":
                    v_low(0, n, 0, bank)
            row_max(0, 0)
            row_max(1, 1)
            dve.wait_ge(first_keys_pool, 1)
            rotate(dve, nc.vector, 0, "qk0", 3, "dve", 2).then_inc(qk_ready, 4)

            def step(i, k, first, last):
                c = i * 16 + k
                t = c * 2
                tail = last and k >= 16
                has_out = not (first and k < 2)
                g = None if tail or (first and k == 0) else group_at(k - 1, 1, last)
                if g and g[1] == "v":
                    v_low(i * 2 + g[3], g[2], g[3] % 2, w_ps[:, :])
                if (k - 1, 1) == LN_SLOT:
                    dve.wait_ge(ln_hi_ready, i + 1)
                    nc.vector.tensor_tensor(ln_lo[:, :, :], w_ps[:, :].rearrange("p (a b) -> p a b", a=CT),
                                            ln_hi[:, :, :].bitcast(F32), ALU.subtract).then_inc(ln_lo_ready, 1)
                if not tail:
                    low_tile(t, 2 * k)
                    if not (last and k == 15):
                        row_max(t + 2, 2 * k + 2)
                if k == 1:
                    variance(LN_COLS, i * LN_STEP + BT)
                if k == 2:
                    newton(i + 2, LN_COLS)
                    normalise(i + 2, ln_x, ln_xn, LN_COLS)
                if has_out:
                    invert(c - 2, 2 * k - 4)
                if not tail:
                    g = group_at(k, 0, last)
                    if g and g[1] == "v":
                        v_low(i * 2 + g[3], g[2], g[3] % 2, w_ps[:, :])
                    if not (last and k == 15):
                        row_max(t + 3, 2 * k + 3)
                if has_out:
                    add_out(c - 2, (k - 2) % 16, (i // 4) if k >= 2 else ((i - 1) // 4))
                if not tail:
                    low_tile(t + 1, 2 * k + 1)
                if not (first and k == 0) and not (last and k == 17):
                    low_out(c - 1, (k - 1) % 2)
                if k == 0:
                    dve.wait_ge(ln_loaded, (i + 1) * 16)
                    mean(i + 2, ln_x, LN_COLS)
                if k in MX_PARTS:
                    quantise(i, MX_PARTS.index(k))

            steps(dve, step)

            def split_gelu(g, f, first):
                dve.wait_ge(gelu_ready, g * FT + f + 1)
                if not (first and f < 4):
                    dve.wait_ge(down_ready, g * FT + f - 3)
                nc.vector.tensor_copy(g_hi[:, f % 4, :], g_full[:, f % 2, :]).then_inc(g_hi_ready, 1)
                dve.wait_ge(g_hi_ready, g * FT + f + 1)
                nc.vector.tensor_tensor(g_lo[:, f % 4, :], g_full[:, f % 2, :], g_hi[:, f % 4, :].bitcast(F32),
                                        ALU.subtract).then_inc(g_lo_ready, 1)

            def sum_rows(g, n, h, rounds):
                if h == 0:
                    dve.wait_ge(y_stored, BATCH * QUARTERS * 16)
                    dve.wait_ge(down_ready, g * FT + FT)
                    dve.wait_ge(y_biased, g + 1)
                    if not (isinstance(rounds, int) and rounds == 0):
                        dve.wait_ge(out_stored[n], rounds * 16)
                rows = slice(2 * h, 2 * h + 2)
                nc.vector.tensor_tensor(y_out[:, n, rows], y_ps[n][:, rows], y_in[:, n, rows], ALU.add).then_inc(rows_ready, 1)

            def group(b, n):
                g, first = b * 2 + n, isinstance(b, int) and b == 0 and n == 0
                for f in range(FT):
                    split_gelu(g, f, first)
                    if f in (1, 2) and not first:
                        sum_rows(g - 1, 1 - n, f - 1, b if n == 1 else b - 1)

            for b in range(2):
                group(b, 0)
                group(b, 1)
            with dve.Fori(2, BATCH) as b:
                group(b, 0)
                group(b, 1)
            for h in range(2):
                sum_rows(GROUPS_FF - 1, 1, h, BATCH - 1)

        @block.tensor
        def _(pe):
            def chain(out, terms, inc=None):
                for n, (w, m) in enumerate(terms):
                    ins = nc.tensor.matmul(out, w, m, start=(n == 0), stop=(n == len(terms) - 1))
                if inc is not None:
                    ins.then_inc(inc, 1)

            def project(part, n, bank):
                if part == "v":
                    cols = PARTS["v"]
                    for t in range(2):
                        tok = slice((2 * n + t) * P, (2 * n + t + 1) * P)
                        chain(bank[:, t * 256:(t + 1) * 256],
                              [term for c in range(CT) for term in
                               ((x_hi[:, c, tok], w_hi[:, c, cols]), (x_hi[:, c, tok], w_lo[:, c, cols]),
                                (x_lo[:, c, tok], w_hi[:, c, cols]))],
                              proj_ready if t == 1 else None)
                    return
                _, kind, half = qk_slot(part, n)
                col = PARTS[part].start + kind * HEAD
                cols, tok = slice(col, col + HEAD), slice(half * HALF, (half + 1) * HALF)
                chain(bank, [term for c in range(CT) for term in
                             ((w_hi[:, c, cols], x_hi[:, c, tok]), (w_hi[:, c, cols], x_lo[:, c, tok]),
                              (w_lo[:, c, cols], x_hi[:, c, tok]))], proj_ready)

            def bank_free(i, k, slot, first, last):
                before = [(k, s) for s in range(slot)][::-1] + [(k - n, s) for n in (1, 2) for s in (2, 1, 0)]
                for kk, s in before:
                    if s == 1:
                        if first and kk < 2:
                            continue
                        pe.wait_ge(y_added, i * 16 + kk - 1)
                        return
                    if (kk, s // 2) == LN_SLOT:
                        pe.wait_ge(ln_lo_ready, i + 1)
                        return
                    if (kk, s // 2) == MX_SLOT:
                        pe.wait_ge(mx_copied, i + 1)
                        return
                    g = group_at(kk % 16, s // 2, last and kk >= 0)
                    if g:
                        p = i * 2 + g[3] - (2 if kk < 0 else 0)
                        if g[1] == "v":
                            pe.wait_ge(v_lo_ready, p * 4 + g[2] + 1)
                        else:
                            pe.wait_ge(rope_in, p * 8 + qk_number(g[1], g[2]) + 1)
                        return

            def scores(k2, p, tile_ready):
                head = (k2 // 8) % 2
                if tile_ready:
                    pe.wait_ge(qk_ready, p * 8 + 4 * (head + 1))
                tile = (k2 % 8) * P
                q_hi, q_lo = qk_hi[:, head, 0, tile:tile + P], qk_lo[:, head, 0, tile:tile + P]
                for h in range(2):
                    keys = slice(h * HALF, (h + 1) * HALF)
                    k_hi, k_lo = qk_hi[:, head, 1, keys], qk_lo[:, head, 1, keys]
                    chain(s_ps[k2 % 2][:, keys], ((q_hi, k_hi), (q_hi, k_lo), (q_lo, k_hi)),
                          scores_ready if h == 1 else None)

            def turn(t, k2, first):
                pe.wait_ge(probs_ready, t + 1)
                for h in range(2):
                    if not first:
                        pe.wait_ge(pt_lo_ready, t * 2 + h - 1)
                    for j in range(4):
                        kt = 4 * h + j
                        ins = nc.tensor.transpose(t_ps[h][:, j, :], probs[:, k2 % 4, kt * P:(kt + 1) * P], ident[:, :])
                    ins.then_inc(pt_ready, 1)

            def values(c, k, p, first):
                pe.wait_ge(pt_lo_ready, c * 4 + 4)
                if not first:
                    pe.wait_ge(o_lo_ready, c)
                if k % 8 == 0:
                    pe.wait_ge(v_lo_ready, p * 4 + 4)
                parity, head, slot = (k // 8) % 2, (k // 4) % 2, k % 2
                cols = slice(head * HEAD, (head + 1) * HEAD)
                chain(o_ps[:, 0:CHUNK],
                      [term for kt in range(BT) for term in
                       ((v_hi[:, parity, kt, cols], pt_hi[:, slot, kt, :]), (v_hi[:, parity, kt, cols], pt_lo[:, slot, kt, :]),
                        (v_lo[:, parity, kt, cols], pt_hi[:, slot, kt, :]))], o_ready)

            def output(c, k, p):
                head, slot = (k // 4) % 2, k % 2
                pe.wait_ge(o_lo_ready, c + 1)
                if k % 4 == 0:
                    pe.wait_ge(wo_lo_ready[head], p + 1)
                for n in range(2):
                    rows = slice(n * P, (n + 1) * P)
                    chain(w_ps[:, n * DIM:(n + 1) * DIM],
                          ((o_hi[:, slot, rows], wo_hi[:, head, :]), (o_hi[:, slot, rows], wo_lo[:, head, :]),
                           (o_lo[:, slot, rows], wo_hi[:, head, :])), out_ready if n == 1 else None)

            down_blocks = down_w.rearrange("p (m f n) -> p m f n", m=CT, f=FT)
            seq_cols = seq_parts[:, :, :, :, :].rearrange("p b h c s -> p (b h c s)")

            def up(b, n, f):
                if isinstance(b, int) and b == 0 and n == 0 and f < 2:
                    if f == 0:
                        pe.wait_ge(mx_w_loaded[0], 16)
                        pe.wait_ge(x_ready, (BATCH + 1) * 32)
                else:
                    pe.wait_ge(gelu_ready, b * 2 * FT + n * FT + f - 1)
                for m in range(2 * CT):
                    c, part = m // 2, m % 2
                    block_at = (2 * f + c) * P
                    at = b * (2 * CT * SEQ) + ((part * CT + c) * SEQ + n * HALF)
                    ins = nc.tensor.matmul(up_ps[f % 2], up_w[:, block_at:block_at + P], seq_cols[:, bass.ds(at, HALF)],
                                           start=(m == 0), stop=(m == 2 * CT - 1))
                ins.then_inc(up_ready, 1)

            def down(b, n, f):
                pe.wait_ge(g_lo_ready, (b * 2 + n) * FT + f + 1)
                if f == 0 and not (isinstance(b, int) and b == 0):
                    pe.wait_ge(rows_ready, (b * 2 + n - 1) * 2)
                for t in range(GT):
                    for m, part in enumerate((g_hi, g_lo)):
                        ins = nc.tensor.matmul(y_ps[n][:, t, :], part[:, f % 4, t * P:(t + 1) * P], down_blocks[:, :, f, :],
                                               start=(f == 0 and m == 0 and t % 2 == 0),
                                               stop=(f == FT - 1 and m == 1 and t % 2 == 1))
                ins.then_inc(down_ready, 1)

            pe.wait_ge(ident_loaded, 16)
            xn_first = probs[:, 0:2, :].rearrange("p a (b c) -> p (a b) c", c=DIM)
            for h in range(2):
                pe.wait_ge(ln_xn_ready, h + 1)
                for c in range(CT):
                    for j in range(4):
                        at = h * HALF + j * P
                        ins = nc.tensor.transpose(s_ps[c][:, at:at + P], xn_first[:, h * 4 + j, c * P:(c + 1) * P], ident[:, :])
                    ins.then_inc(first_turned, 1)
            for m, ((place, part, n), bank) in enumerate(zip(FIRST_GROUPS, FIRST_BANKS)):
                pe.wait_ge(w_lo_ready[part], 1)
                if m < 2:
                    pe.wait_ge(x_ready, 16 * (m + 1))
                if m in FIRST_HELD:
                    pe.wait_ge(rope_in, FIRST_GROUPS[FIRST_HELD[m]][2] + 1)
                project(part, n, bank)
            pe.wait_ge(first_qk_dve, 2)
            pe.wait_ge(first_keys_pool, 1)
            scores(0, 0, False)
            pe.wait_ge(rope_in, 6)
            pe.wait_ge(v_lo_ready, 1)
            scores(1, 0, False)

            def step(i, k, first, last):
                c = i * 16 + k
                t = c * 2
                tail = last and k >= 16

                def next_scores(n):
                    if last and k == 15:
                        return
                    k2 = 2 * k + 2 + n
                    scores(k2, i * 2 + k2 // 16, k2 % 8 == 0 or (first and k2 == 4))

                def slot(n):
                    if (k, n) == LN_SLOT:
                        bank_free(i, k, 2 * n, first, last)
                        pe.wait_ge(ln_xn_ready, i + 3)
                        for m in range(CT * LN_STEP):
                            ins = nc.tensor.transpose(w_ps[:, m * P:(m + 1) * P],
                                                      ln_xn[:, m % LN_STEP, (m // LN_STEP) * P:(m // LN_STEP + 1) * P], ident[:, :])
                        ins.then_inc(ln_turned, 1)
                        return
                    if (k, n) == MX_SLOT:
                        bank_free(i, k, 2 * n, first, last)
                        pe.wait_ge(mx_ready, i + 1)
                        for m in range(MX_STEP // P):
                            ins = nc.tensor.transpose(w_ps[:, m * P:(m + 1) * P], mx_q[:, m * P:(m + 1) * P], ident[:, :])
                        ins.then_inc(mx_turned_ready, 1)
                        return
                    g = group_at(k, n, last)
                    if not g:
                        return
                    place, part, num, ahead = g
                    if first and k == 0:
                        pe.wait_ge(rope_in, 6)
                        pe.wait_ge(v_lo_ready, 4)
                    else:
                        bank_free(i, k, 2 * n, first, last)
                    if num == 0:
                        pe.wait_ge(w_lo_ready[part], i * 2 + ahead + 1)
                    if place == 0 and ahead == 2:
                        pe.wait_ge(x_ready, ((i + 1) // 4 + 1) * 32)
                    project(part, num, w_ps[:, :])

                if tail:
                    up(0, 0, k - 16)
                if not tail:
                    turn(t, 2 * k, first and k == 0)
                    next_scores(0)
                    slot(0)
                    turn(t + 1, 2 * k + 1, False)
                    next_scores(1)
                if not (first and k < 2):
                    bank_free(i, k, 1, first, last)
                    output(c - 2, (k - 2) % 16, i * 2 + (k - 2) // 8)
                if not (first and k == 0) and not (last and k == 17):
                    values(c - 1, (k - 1) % 16, i * 2 + (k - 1) // 8, first and k == 1)
                if not tail:
                    slot(1)

            steps(pe, step)

            def group(b, n, final):
                for f in range(FT):
                    if f < FT - 2:
                        up(b, n, f + 2)
                    elif n == 0:
                        up(b, 1, f + 2 - FT)
                    elif not final:
                        up(b + 1, 0, f + 2 - FT)
                    down(b, n, f)

            pe.wait_ge(mx_w_loaded[1], 16)
            group(0, 0, False)
            pe.wait_ge(seq_loaded[1], 32)
            group(0, 1, False)
            with pe.Fori(1, BATCH - 1) as b:
                group(b, 0, False)
                for n in range(2, BATCH):
                    pe.wait_ge(seq_loaded[n], 32)
                group(b, 1, False)
            group(BATCH - 1, 0, False)
            group(BATCH - 1, 1, True)


def _rope_tables():
    inv = (np.float32(1.0) / np.power(np.float32(10000.0), np.arange(0, HEAD, 2, dtype=np.float32) / np.float32(HEAD))).astype(np.float32)
    angle = (np.arange(SEQ, dtype=np.float32)[None, :] * inv[:, None]).astype(np.float32)
    cos, sin = np.cos(angle.astype(np.float64)), np.sin(angle.astype(np.float64))
    return np.concatenate([cos, cos]).astype(np.float32), np.concatenate([-sin, sin]).astype(np.float32)


def build(nc, ins, outs):
    d = dict(ins)
    d["xnt"] = nc.dram_tensor("xnt_parts", [2, P, CT, TOK], F32, kind="Internal").ap()
    d["mx"] = nc.dram_tensor("mx_blocks", [P, MX_COLS], F32, kind="Internal").ap()
    d["y"] = nc.dram_tensor("x_plus_attention", [P, TILES, DIM], F32, kind="Internal").ap()
    d["out"] = outs["out"].rearrange("(t p) c -> p t c", p=P)
    d["x"] = ins["x"].rearrange("(t p) c -> p t c", p=P)
    layer(nc, d)


def kernel(L0_attn_x, L0_attn_w_qkv, L0_attn_w_out, L0_ffn_up_kernel, L0_ffn_up_bias, L0_ffn_down_kernel, L0_ffn_down_bias):
    import concourse.bacc as bacc
    from concourse.bass_utils import run_bass_kernel_spmd

    A = np.ascontiguousarray
    cos, sin = _rope_tables()
    w = np.asarray(L0_attn_w_qkv).reshape(3, HEADS // 2, 2, HEAD, CT, P)
    cols = [w[0, :, 0], w[1, :, 0], w[0, :, 1], w[1, :, 1], w[2, :, 0], w[2, :, 1]]
    w_qkv = np.concatenate(cols, axis=1).transpose(0, 3, 2, 1)
    w_out = np.asarray(L0_attn_w_out).reshape(DIM, HEADS // 2, 2, HEAD).transpose(1, 3, 2, 0)
    arrays = {
        "x": A(np.asarray(L0_attn_x).reshape(TOK, DIM)),
        "w_qkv": A(w_qkv),
        "w_out": A(w_out),
        "mx_rows": A(np.concatenate([
            np.asarray(L0_ffn_up_kernel).T.reshape(FT, P, DIM).transpose(1, 0, 2).reshape(P, FT * DIM),
            np.asarray(L0_ffn_down_kernel).T.reshape(CT, P, FF).transpose(1, 0, 2).reshape(P, CT * FF)], axis=1)),
        "up_bias": A(np.asarray(L0_ffn_up_bias).reshape(FT, P).T),
        "down_bias": A(np.asarray(L0_ffn_down_bias).reshape(1, DIM)),
        "cos": cos, "sin": sin, "ident": np.eye(P, dtype=np.float32),
    }
    nc = bacc.Bacc("TRN2", target_bir_lowering=False, num_devices=1)
    ins = {n: nc.dram_tensor(f"in_{n}", a.shape, mybir.dt.from_np(a.dtype), kind="ExternalInput").ap() for n, a in arrays.items()}
    outs = {"out": nc.dram_tensor("out_dram", (TOK, DIM), F32, kind="ExternalOutput").ap()}
    build(nc, ins, outs)
    r = run_bass_kernel_spmd(nc, [{f"in_{n}": a for n, a in arrays.items()}], core_ids=[0])
    return r.results[0]["out_dram"].reshape(BATCH, SEQ, DIM)
```
